# Optimizing a Trainium2 kernel written in Bass

```python
import numpy as np
import jax
import jax.numpy as jnp

def _softmax(x, axis=-1):
    return jax.nn.softmax(x, axis=axis)

def _gelu(x):
    return jax.nn.gelu(x, approximate=True)

def _silu(x):
    return jax.nn.silu(x)

def _sigmoid(x):
    return jax.nn.sigmoid(x)

def _layernorm(x, axis=-1, eps=1e-05):
    m = jnp.mean(x, axis=axis, keepdims=True)
    v = jnp.var(x, axis=axis, keepdims=True)
    return (x - m) / jnp.sqrt(v + eps)

def _scatter_add(tgt, idx, src, axis=0):
    return tgt.at[idx].add(src)

def _segment_sum(src, seg, n):
    return jax.ops.segment_sum(src, seg, n)
kernel_name = 'mk_early_fusion_d1_tok_img768_r4_755968'

def setup_inputs(seed: int=0):
    np.random.seed(seed)
    _w = jnp.asarray

    def _rec_inputs():
        import jax
        import jax.numpy as jnp
        _rk = jax.random.key(seed)
        x = -0.000222058 + 0.999998 * jax.random.normal(jax.random.fold_in(_rk, 1), (32, 64, 64, 3), jnp.float32)
        txt = -0.00015822 + 0.554492 * jax.random.normal(jax.random.fold_in(_rk, 2), (32, 32, 192), jnp.float32)
        return (x, txt)
    x, txt = _rec_inputs()

    def _L0_tok_setup():
        import jax, jax.numpy as jnp
        import numpy as np
        PATCH = 16

        def _extract_patches(x, p):
            B, H, W, C = x.shape
            x = x.reshape(B, H // p, p, W // p, p, C)
            x = x.transpose(0, 1, 3, 2, 4, 5)
            return x.reshape(B, H // p * (W // p), p * p * C)
        key = jax.random.key(seed)
        k1, k2, k3 = jax.random.split(key, 3)
        B, H, W, C = (128, 64, 64, 3)
        patch_dim = PATCH * PATCH * C
        hidden = 192
        n_patches = H // PATCH * (W // PATCH)
        x = jax.random.normal(k1, (B, H, W, C), dtype=jnp.float32)
        Wp = jax.random.normal(k2, (patch_dim, hidden), dtype=jnp.float32) * 0.02
        b = jnp.zeros((hidden,), dtype=jnp.float32)
        pos_emb = jax.random.normal(k3, (n_patches, hidden), dtype=jnp.float32) * 0.02
        return {'x': x, 'W': Wp, 'b': b, 'pos_emb': pos_emb}
    _L0_tok_all = _L0_tok_setup()
    _L0_tok_in = {k: v for k, v in _L0_tok_all.items() if k in ('W', 'b', 'pos_emb')}
    del _L0_tok_all

    def _L0_attn_setup():
        import jax, jax.numpy as jnp
        import numpy as np
        ROPE_THETA = 10000.0

        def rope(x):
            B, S, D = x.shape
            half = D // 2
            inv_freq = 1.0 / ROPE_THETA ** (jnp.arange(half, dtype=jnp.float32) * 2.0 / D)
            ang = jnp.arange(S, dtype=jnp.float32)[:, None] * inv_freq[None, :]
            cos, sin = (jnp.cos(ang), jnp.sin(ang))
            x1, x2 = (x[..., 0::2], x[..., 1::2])
            r1 = x1 * cos - x2 * sin
            r2 = x1 * sin + x2 * cos
            return jnp.stack([r1, r2], axis=-1).reshape(B, S, D)
        key = jax.random.key(seed)
        ks = jax.random.split(key, 9)
        B, S, D = (4, 512, 192)
        w = 0.02
        return {'X': jax.random.normal(ks[0], (B, S, D), dtype=jnp.float32), 'Wq': jax.random.normal(ks[1], (D, D), dtype=jnp.float32) * w, 'bq': jnp.zeros((D,), dtype=jnp.float32), 'Wk': jax.random.normal(ks[2], (D, D), dtype=jnp.float32) * w, 'bk': jnp.zeros((D,), dtype=jnp.float32), 'Wv': jax.random.normal(ks[3], (D, D), dtype=jnp.float32) * w, 'bv': jnp.zeros((D,), dtype=jnp.float32), 'Wo': jax.random.normal(ks[4], (D, D), dtype=jnp.float32) * w, 'bo': jnp.zeros((D,), dtype=jnp.float32)}
    _L0_attn_all = _L0_attn_setup()
    _L0_attn_in = {k: v for k, v in _L0_attn_all.items() if k in ('Wq', 'bq', 'Wk', 'bk', 'Wv', 'bv', 'Wo', 'bo')}
    del _L0_attn_all

    def _L0_ffn_setup():
        import jax, jax.numpy as jnp
        import numpy as np
        import math
        B, S, D = (4, 1024, 192)
        E = 8
        TOP_K = 2
        H = 512
        CAP_F = 1.25
        EPS = 1e-06
        ALPHA = 1.0
        key = jax.random.key(seed)
        k0, k1, k2, k3 = jax.random.split(key, 4)
        x = jax.random.normal(k0, (B, S, D), jnp.float32)
        gate_w = jax.random.normal(k1, (E, D), jnp.float32) * 0.02
        w13 = jax.random.normal(k2, (E, 2 * H, D), jnp.float32) * 0.02
        w2 = jax.random.normal(k3, (E, D, H), jnp.float32) * 0.02
        norm_w = jnp.ones((E, D), jnp.float32)
        return {'x': x, 'gate_w': gate_w, 'w13': w13, 'w2': w2, 'norm_w': norm_w}
    _L0_ffn_all = _L0_ffn_setup()
    _L0_ffn_in = {k: v for k, v in _L0_ffn_all.items() if k in ('gate_w', 'w13', 'w2', 'norm_w')}
    del _L0_ffn_all
    return {'x': x, 'txt': txt, 'L0_tok_W': _L0_tok_in['W'], 'L0_tok_b': _L0_tok_in['b'], 'L0_tok_pos_emb': _L0_tok_in['pos_emb'], 'L0_attn_Wq': _L0_attn_in['Wq'], 'L0_attn_bq': _L0_attn_in['bq'], 'L0_attn_Wk': _L0_attn_in['Wk'], 'L0_attn_bk': _L0_attn_in['bk'], 'L0_attn_Wv': _L0_attn_in['Wv'], 'L0_attn_bv': _L0_attn_in['bv'], 'L0_attn_Wo': _L0_attn_in['Wo'], 'L0_attn_bo': _L0_attn_in['bo'], 'L0_ffn_gate_w': _L0_ffn_in['gate_w'], 'L0_ffn_w13': _L0_ffn_in['w13'], 'L0_ffn_w2': _L0_ffn_in['w2'], 'L0_ffn_norm_w': _L0_ffn_in['norm_w']}

def reference(x, txt, L0_tok_W, L0_tok_b, L0_tok_pos_emb, L0_attn_Wq, L0_attn_bq, L0_attn_Wk, L0_attn_bk, L0_attn_Wv, L0_attn_bv, L0_attn_Wo, L0_attn_bo, L0_ffn_gate_w, L0_ffn_w13, L0_ffn_w2, L0_ffn_norm_w):
    import jax
    import jax.numpy as jnp

    def _L0_tok_ref(x, W, b, pos_emb):
        import jax, jax.numpy as jnp
        import numpy as np
        PATCH = 16

        def _extract_patches(x, p):
            B, H, W, C = x.shape
            x = x.reshape(B, H // p, p, W // p, p, C)
            x = x.transpose(0, 1, 3, 2, 4, 5)
            return x.reshape(B, H // p * (W // p), p * p * C)
        patches = _extract_patches(x, PATCH)
        proj = jnp.einsum('bnd,dh->bnh', patches, W) + b
        return proj + pos_emb[None, :, :]

    def _L0_attn_ref(X, Wq, bq, Wk, bk, Wv, bv, Wo, bo):
        import jax, jax.numpy as jnp
        import numpy as np
        ROPE_THETA = 10000.0

        def rope(x):
            B, S, D = x.shape
            half = D // 2
            inv_freq = 1.0 / ROPE_THETA ** (jnp.arange(half, dtype=jnp.float32) * 2.0 / D)
            ang = jnp.arange(S, dtype=jnp.float32)[:, None] * inv_freq[None, :]
            cos, sin = (jnp.cos(ang), jnp.sin(ang))
            x1, x2 = (x[..., 0::2], x[..., 1::2])
            r1 = x1 * cos - x2 * sin
            r2 = x1 * sin + x2 * cos
            return jnp.stack([r1, r2], axis=-1).reshape(B, S, D)
        NUM_HEADS = 12
        B, S, D = X.shape
        hd = D // NUM_HEADS
        q = rope(X @ Wq + bq)
        k = rope(X @ Wk + bk)
        v = X @ Wv + bv
        qh = q.reshape(B, S, NUM_HEADS, hd)
        kh = k.reshape(B, S, NUM_HEADS, hd)
        vh = v.reshape(B, S, NUM_HEADS, hd)
        scores = jnp.einsum('bqhd,bkhd->bhqk', qh, kh) / jnp.sqrt(jnp.float32(hd))
        causal = jnp.tril(jnp.ones((S, S), dtype=bool))
        scores = jnp.where(causal[None, None, :, :], scores, -jnp.inf)
        weights = jax.nn.softmax(scores, axis=-1)
        out = jnp.einsum('bhqk,bkhd->bqhd', weights, vh).reshape(B, S, D)
        return out @ Wo + bo

    def _L0_ffn_ref(x, gate_w, w13, w2, norm_w):
        import jax, jax.numpy as jnp
        import numpy as np
        import math
        B, S, D = (4, 1024, 192)
        E = 8
        TOP_K = 2
        H = 512
        CAP_F = 1.25
        EPS = 1e-06
        ALPHA = 1.0
        Bx, Sx, Dx = x.shape
        N = Bx * Sx
        cap = int(math.ceil(CAP_F * TOP_K * N / E))
        xf = x.reshape(N, Dx)
        logits = xf.astype(jnp.float32) @ gate_w.T
        probs = jax.nn.softmax(logits, axis=-1)
        top_p, top_i = jax.lax.top_k(probs, TOP_K)
        w = top_p / jnp.sum(top_p, axis=-1, keepdims=True)
        flat_e = top_i.reshape(-1)
        onehot = jax.nn.one_hot(flat_e, E, dtype=jnp.int32)
        pos = jnp.take_along_axis(jnp.cumsum(onehot, axis=0) - 1, flat_e[:, None], axis=1)[:, 0]
        keep = pos < cap
        didx = flat_e * cap + jnp.minimum(pos, cap - 1)
        safe = jnp.where(keep, didx, E * cap)
        x_rep = jnp.repeat(xf, TOP_K, axis=0)
        buf = jnp.zeros((E * cap + 1, Dx), x.dtype).at[safe].set(x_rep)
        buf = buf[:-1].reshape(E, cap, Dx)
        z = 2.0 * buf
        z = z * jax.lax.rsqrt(jnp.mean(z * z, axis=-1, keepdims=True) + EPS)
        z = z * norm_w[:, None, :]
        gu = jnp.einsum('ecd,ehd->ech', z, w13)
        g, u = jnp.split(gu, 2, axis=-1)
        y = buf + ALPHA * jnp.einsum('ech,edh->ecd', jax.nn.silu(g) * u, w2)
        y_tok = y.reshape(E * cap, Dx)[didx]
        cw = (w.reshape(-1) * keep.astype(w.dtype)).astype(x.dtype)
        out = (cw[:, None] * y_tok).reshape(N, TOP_K, Dx).sum(axis=1)
        return out.reshape(Bx, Sx, Dx)
    h = _L0_tok_ref(x, L0_tok_W, L0_tok_b, L0_tok_pos_emb)
    h = jnp.concatenate([h, txt], axis=1)
    h = h + _L0_attn_ref(_layernorm(h, axis=-1), L0_attn_Wq, L0_attn_bq, L0_attn_Wk, L0_attn_bk, L0_attn_Wv, L0_attn_bv, L0_attn_Wo, L0_attn_bo)
    h = h + _L0_ffn_ref(_layernorm(h, axis=-1), L0_ffn_gate_w, L0_ffn_w13, L0_ffn_w2, L0_ffn_norm_w)
    return h

_drawn_inputs = setup_inputs


def setup_inputs(seed=0):
    import zlib

    import numpy as np

    out = dict(_drawn_inputs(seed))
    spreads = {'L0_tok_b': (0.0, 0.1),
     'L0_attn_bq': (0.0, 0.8),
     'L0_attn_bk': (0.0, 0.8),
     'L0_attn_bv': (0.0, 0.1),
     'L0_attn_bo': (0.0, 0.1),
     'L0_ffn_norm_w': (1.0, 0.6)}
    factors = {'L0_attn_Wq': 8.0, 'L0_attn_Wk': 8.0, 'L0_ffn_w13': 6.339, 'L0_ffn_w2': 6.264}
    for name, (base, spread) in spreads.items():
        noise = np.random.default_rng([zlib.crc32(name.encode()), seed]).standard_normal(out[name].shape)
        drawn = base * np.exp(spread * noise) if base else spread * noise
        out[name] = jnp.asarray(drawn.astype(out[name].dtype))
    for name, factor in factors.items():
        out[name] = (out[name] * factor).astype(out[name].dtype)
    return out
```

```python
from contextlib import ExitStack

import numpy as np

import concourse.bass as bass
from concourse import mybir

F32 = mybir.dt.float32
BF16 = mybir.dt.bfloat16
U32 = mybir.dt.uint32
ALU = mybir.AluOpType
ACT = mybir.ActivationFunctionType
AX = mybir.AxisListType

P = 128
B, IMG, PATCH, CH = 32, 64, 16, 3
NPATCH = (IMG // PATCH) ** 2
PDIM = PATCH * PATCH * CH
PK = PDIM // P
NTXT = 32
S = NPATCH + NTXT
D = 192
D0, D1 = P, D - P
HEADS, HD = 12, 16
HG = HEADS // 4
NT = B // 2
HALF = 64
N = B * S
E, H = 8, 512
MH = H // P
CAP = -(-5 * 2 * N // (4 * E))
CC, CR = 4, CAP // 4
ROW = D + 4
W_COL, ID_COL, RMS_COL = D, D + 1, D + 2
SPP = E * CAP // P
FAR = 1.0e5
LN_EPS, RMS_EPS = 1e-5, 1e-6
assert CAP == 480 and N == 1536


def shape_constants():
    c = {}
    half = D // 2
    inv = (1.0 / np.float32(10000.0) ** (np.arange(half, dtype=np.float32) * np.float32(2.0) / np.float32(D))).astype(np.float32)
    ang = (np.arange(S, dtype=np.float32)[:, None] * inv[None, :]).astype(np.float32)
    cos, sin = np.cos(ang), np.sin(ang)
    cos2 = np.repeat(cos, 2, axis=1)
    sin2 = np.stack([-sin, sin], axis=-1).reshape(S, D)
    rope = np.zeros((P, 2, 2, D), np.float32)
    mask = np.zeros((P, S), np.float32)
    causal = np.where(np.tril(np.ones((S, S), bool)), 0.0, -1.0e30).astype(np.float32)
    for lo in (0, HALF):
        for j, scale in ((0, HD ** -0.5), (1, 1.0)):
            rope[lo:lo + S, 0, j] = cos2 * scale
            rope[lo:lo + S, 1, j] = sin2 * scale
        mask[lo:lo + S] = causal
    c["rope"] = rope.reshape(P, -1)
    c["mask"] = np.tile(mask, (1, HEADS))
    live = np.zeros(P, bool)
    live[:S] = live[HALF:HALF + S] = True
    rev = np.tile(np.arange(E, 0, -1, dtype=np.float32), (P, 1))
    gap = np.where(live, 0.0, FAR).astype(np.float32)[:, None]
    ids = np.full((P, NT), FAR, np.float32)
    for t in range(NT):
        ids[0:S, t] = (2 * t) * S + np.arange(S)
        ids[HALF:HALF + S, t] = (2 * t + 1) * S + np.arange(S)
    power = np.full((P, NT), -0.5, np.float32)
    power = np.concatenate([power, np.full((P, 1), RMS_EPS, np.float32), np.full((P, 2), 2.0, np.float32)], axis=1)
    spare = (N + np.arange(E * CAP) % CAP).reshape(P, SPP).astype(np.float32)
    c["small"] = np.concatenate([rev, gap, power, ids, spare], axis=1)
    before = (np.arange(P)[:, None] < np.arange(P)[None, :]) & live[:, None]
    every = np.repeat(live[:, None], P, axis=1)
    c["order"] = np.concatenate([before, every], axis=1).astype(np.float32)
    c["ident"] = np.eye(P, dtype=np.float32)
    return c


REV0, GAP0, POW0 = 0, E, E + 1
EPS0 = POW0 + NT
TWO0 = EPS0 + 1
IDS0 = TWO0 + 2
SPARE0 = IDS0 + NT
SMALL = SPARE0 + SPP

PEEL = 6

STEPS = {"B": 1, "C": 4, "D": 22}


def build(nc, patches, txt, posb, tokb, tokw, wqkv, wo, gate, w13, w2, normw,
          rope, mask, small, order, ident, out):
    slots = nc.dram_tensor("slots", (E * CAP, ROW), F32, kind="Internal").ap()
    fused = nc.dram_tensor("patch_tokens", (B * NPATCH, D), F32, kind="Internal").ap()
    with ExitStack() as ctx:
        def sb(name, shape, dt=F32):
            return ctx.enter_context(nc.sbuf_tensor(name, shape, dt))

        def sem(name):
            return ctx.enter_context(nc.semaphore(name))

        ident_sb = sb("ident_sb", [P, P])
        rope_sb = sb("rope_sb", [P, 2, 2 * D])
        mask_sb = sb("mask_sb", [P, HEADS, S])
        small_sb = sb("small_sb", [P, SMALL])
        orderf_sb = sb("orderf_sb", [P, 2 * P])
        order_sb = sb("order_sb", [P, 2 * P], BF16)
        tokw_sb = sb("tokw_sb", [P, PK, D])
        patch_sb = sb("patch_sb", [P, PK, B * NPATCH])
        posb_sb = sb("posb_sb", [P, D])
        tokb_sb = sb("tokb_sb", [P, D])
        ptok_sb = sb("ptok_sb", [P, 4, D])
        wqkv0_sb = sb("wqkv0_sb", [P, 3 * D])
        wqkv1_sb = sb("wqkv1_sb", [D1 + 1, 3 * D])
        wo0_sb = sb("wo0_sb", [P, D])
        wo1_sb = sb("wo1_sb", [D1 + 1, D])
        gate_sb = sb("gate_sb", [P, 2, E])
        zero_sb = sb("zero_sb", [P, SPP, ROW])
        h_all = sb("h_all", [P, NT, D])
        stats = sb("stats", [P, NT, 6])
        mv = sb("mv", [P, NT, 2])
        ve1 = sb("ve1", [P, NT])
        rstd1 = sb("rstd1", [P, NT])
        xn = sb("xn", [P, D])
        xT0 = sb("xT0", [P, 2, 2, HALF])
        xT1 = sb("xT1", [D1 + 1, 2, 2, HALF])
        rc = sb("rc", [P, 2 * D])
        rs = sb("rs", [P, 2 * D])
        qk = sb("qk", [P, 2, HEADS, 32])
        qkT = sb("qkT", [P, 2, 2, HG, P])
        vbd = sb("vbd", [P, 2, 2, HEADS // 2, 2, HD + 1])
        sm = sb("sm", [P, HEADS * S])
        mx = sb("mx", [P, HEADS])
        pr = sb("pr", [P, HEADS, 64])
        pT = sb("pT", [P, 2, HEADS // 2, P])
        rden = sb("rden", [P, HEADS])
        att = sb("att", [P, D])
        oT0 = sb("oT0", [P, P])
        oT1 = sb("oT1", [D1 + 1, P])
        st2 = sb("st2", [P, 6])
        mv2 = sb("mv2", [P, 2])
        ve2 = sb("ve2", [P, 1])
        rstd2 = sb("rstd2", [P, 1])
        x2 = sb("x2", [P, 2, D])
        x2T0 = sb("x2T0", [P, P])
        x2T1 = sb("x2T1", [D1, P])
        squares = sb("squares", [P, D])
        ssq = sb("ssq", [P, 1])
        ms = sb("ms", [P, 1])
        rms = sb("rms", [P, 1])
        lg = sb("lg", [P, E])
        lg2 = sb("lg2", [P, E])
        top = sb("top", [P, 2])
        cand = sb("cand", [P, 2, E])
        rank = sb("rank", [P, 2])
        hot = sb("hot", [P, 2, E])
        hots = sb("hots", [P, E], BF16)
        pos = sb("pos", [P, E])
        count = sb("count", [P, E])
        posk = sb("posk", [P, 2, E])
        pk = sb("pk", [P, 2])
        base = sb("base", [P, 2])
        over = sb("over", [P, 2])
        keep = sb("keep", [P, 2])
        gapd = sb("gapd", [P, 1])
        ratio = sb("ratio", [P, 1])
        total = sb("total", [P, 1])
        wts = sb("wts", [P, 2])
        slot = sb("slot", [P, 2, 2], U32)
        row = sb("row", [P, 2, 2, ROW])
        w13a_sb = sb("w13a_sb", [P, 2, 2 * H])
        w13b_sb = sb("w13b_sb", [D1, 2, 2 * H])
        w2_sb = sb("w2_sb", [P, 2, MH, D])
        nw0_sb = sb("nw0_sb", [P, E])
        nw1_sb = sb("nw1_sb", [D1, E])
        zs = sb("zs", [CR, 2, CC, ROW])
        zn = sb("zn", [CR, CC, D])
        z0 = sb("z0", [P, 2, CAP])
        z1 = sb("z1", [D1, 2, CAP])
        sg = sb("sg", [P, 2, CAP])
        hT = sb("hT", [P, MH, CAP])
        yx = sb("yx", [CR, CC, D])
        yw = sb("yw", [CR, CC, D])
        tok = sb("tok", [CR, 2, CC], U32)

        bank = [ctx.enter_context(nc.psum_tensor(f"bank{i}", [P, 512], F32)) for i in range(8)]

        s_patch = sem("patch_in"); s_tokw = sem("tokw_in"); s_posb = sem("posb_in")
        s_const = sem("const_in"); s_wqkv = sem("wqkv_in"); s_wo = sem("wo_in")
        s_txt = sem("txt_in"); s_slots0 = sem("slots_cleared"); s_ptok_out = sem("patch_tokens_out")
        s_ptok_in = sem("patch_tokens_in"); s_h_out = sem("h_out")
        s_zero = sem("zero_ready"); s_gaps = sem("gaps_ready"); s_ones = sem("ones_ready")
        s_pe_tok = sem("patch_product"); s_posum = sem("pos_bias_sum"); s_ptok = sem("patch_tokens_ready")
        s_order = sem("order_bf16"); s_stat = sem("stats_ready"); s_rstd1 = sem("rstd1_ready")
        s_pre = sem("vector_pre_step")
        s_xn = sem("xn_ready"); s_xt = sem("xn_turned"); s_xT = sem("xT_ready")
        s_qkv = sem("qkv_product"); s_rope = sem("rope_parts"); s_qk = sem("qk_ready")
        s_v = sem("v_ready"); s_qkt = sem("qk_turned"); s_qkT = sem("qkT_ready")
        sA = sem("vector_step_A")
        s_sc = sem("scores"); s_sh = sem("scores_shifted"); s_exp = sem("exp_ready")
        s_pt = sem("probs_turned"); s_pT = sem("pT_ready"); sB = sem("vector_step_B")
        s_scread = sem("scores_read")
        s_pv = sem("values_product"); s_att = sem("attention_ready"); s_ot = sem("attention_turned")
        s_oT = sem("oT_ready"); s_proj = sem("projection"); s_var2 = sem("variance2_ready")
        s_rstd2 = sem("rstd2_ready"); s_x2 = sem("x2_ready"); sC = sem("vector_step_C")
        s_x2t = sem("x2_turned"); s_x2T = sem("x2T_ready"); s_ssq = sem("square_sum")
        s_ms = sem("mean_square"); s_rms = sem("rms_ready"); s_gate = sem("logits")
        s_diff = sem("logit_gap"); s_ratio = sem("ratio_ready"); s_hots = sem("hots_ready")
        s_pos = sem("positions"); s_slot = sem("slot_ready"); s_rowx = sem("row_x_ready"); s_rowid = sem("row_index_ready")
        s_disp = [sem("dispatched_even"), sem("dispatched_odd")]; sD = sem("vector_step_D")
        s_w = [sem("expert_weights_even"), sem("expert_weights_odd")]; s_nw = sem("norm_w_in")
        s_zs = [sem("slots_in_even"), sem("slots_in_odd")]
        s_zn = sem("z_scaled"); s_zt = sem("z_turned"); s_z = sem("z_ready")
        s_up = sem("up_product"); s_silu = sem("silu_ready"); s_hT = sem("hidden_ready")
        s_down = sem("down_product"); s_yx = sem("y_plus_x"); s_yw = sem("y_weighted")
        s_tok = sem("token_index"); s_add = sem("added")

        block = ctx.enter_context(nc.Block())

        def pipeline(eng, iteration):
            for i in range(PEEL):
                iteration(i, i, i % 2, *[i >= k for k in range(4)])
            with eng.Fori(PEEL // 2, NT // 2 - 1) as turn:
                iteration(turn * 2, PEEL, 0, True, True, True, True)
                iteration(turn * 2 + 1, PEEL, 1, True, True, True, True)
            for i in range(NT - 2, NT + 3):
                iteration(i, i, i % 2, *[i - k < NT for k in range(4)])

        @block.sync
        def _(sp):
            sp.dma_start(patch_sb[:, 0:3, :], patches[:, 0:3, :]).then_inc(s_patch, 16)
            sp.dma_start(tokw_sb[:, :, :], tokw).then_inc(s_tokw, 16)
            sp.dma_start(patch_sb[:, 3:6, :], patches[:, 3:6, :]).then_inc(s_patch, 16)
            sp.dma_start(posb_sb[:, :], posb).then_inc(s_posb, 16)
            sp.dma_start(tokb_sb[:, :], tokb).then_inc(s_posb, 16)
            sp.dma_start(ident_sb[:, :], ident).then_inc(s_const, 16)
            sp.wait_ge(s_gaps, 1)
            tx = txt.rearrange("(t two) s d -> two s t d", two=2)
            for two in range(2):
                at = two * HALF + NPATCH
                sp.dma_start(h_all[at:at + NTXT, :, :], tx[two]).then_inc(s_txt, 16)
            sp.dma_start(rope_sb[:, :, :], rope.rearrange("p (a b) -> p a b", a=2)).then_inc(s_const, 16)
            sp.dma_start(mask_sb[:, :, :], mask.rearrange("p (a b) -> p a b", a=HEADS)).then_inc(s_const, 16)
            sp.dma_start(small_sb[:, :], small).then_inc(s_const, 16)
            sp.dma_start(orderf_sb[:, :], order).then_inc(s_const, 16)
            sp.dma_start(wqkv0_sb[:, :], wqkv[0:P, :]).then_inc(s_wqkv, 16)
            sp.dma_start(wqkv1_sb[:, :], wqkv[P:D + 1, :]).then_inc(s_wqkv, 16)
            sp.dma_start(wo0_sb[:, :], wo[0:P, :]).then_inc(s_wo, 16)
            sp.dma_start(wo1_sb[:, :], wo[P:D + 1, :]).then_inc(s_wo, 16)
            sp.dma_start(gate_sb[:, 0, :], gate[0:P, :]).then_inc(s_wo, 16)
            sp.dma_start(gate_sb[0:D1, 1, :], gate[P:D, :]).then_inc(s_wo, 16)
            sp.wait_ge(s_ptok, 4)
            sp.dma_start(fused.rearrange("(g p) d -> p g d", p=P), ptok_sb[:, :, :]).then_inc(s_ptok_out, 16)
            sp.wait_ge(s_ptok_out, 16)
            fu = fused.rearrange("(t two s) d -> two s t d", two=2, s=NPATCH)
            for two in range(2):
                sp.dma_start(h_all[two * HALF:two * HALF + NPATCH, :, :], fu[two]).then_inc(s_ptok_in, 16)
            sp.wait_ge(s_zero, 1)
            sp.dma_start(slots.rearrange("(p r) c -> p r c", p=P), zero_sb[:, :, :]).then_inc(s_slots0, 16)
            sp.dma_start(out[N:N + CAP, :].rearrange("(c p) d -> p c d", p=CR),
                         zero_sb[0:CR, 0:CC, 0:D]).then_inc(s_h_out, 16)
            sp.dma_start(nw0_sb[:, :], normw[0:P, :]).then_inc(s_nw, 16)
            sp.dma_start(nw1_sb[:, :], normw[P:D, :]).then_inc(s_nw, 16)

            def load_weights(e, par):
                sp.dma_start(w13a_sb[:, par, :], w13[bass.ds(e * D, P), :]).then_inc(s_w[par], 16)
                sp.dma_start(w13b_sb[:, par, :], w13[bass.ds(e * D + P, D1), :]).then_inc(s_w[par], 16)
                sp.dma_start(w2_sb[:, par, :, :],
                             w2[bass.ds(e * H, H), :].rearrange("(m p) d -> p m d", p=P)).then_inc(s_w[par], 16)

            def load_slots(e, par):
                sp.dma_start(zs[:, par, :, :],
                             slots[bass.ds(e * CAP, CAP), :].rearrange("(c p) r -> p c r", p=CR)).then_inc(s_zs[par], 16)

            load_weights(0, 0)
            load_weights(1, 1)
            sp.wait_ge(s_x2, NT)
            ho = out[0:N, :].rearrange("(b s) d -> b s d", s=S).rearrange("(t two) s d -> two s t d", two=2)
            for two in range(2):
                sp.dma_start(ho[two], h_all[two * HALF:two * HALF + S, :, :]).then_inc(s_h_out, 16)
            for par in range(2):
                sp.wait_ge(s_disp[par], 32 * NT // 2)
            load_slots(0, 0)
            load_slots(1, 1)
            with sp.Fori(1, E // 2) as pair:
                for par in range(2):
                    e = pair * 2
                    sp.wait_ge(s_down, 2 * (e + (par - 1)))
                    load_weights(e + par, par)
                    sp.wait_ge(s_yw, CC * (e + (par - 1)))
                    sp.wait_ge(s_tok, e + (par - 1))
                    load_slots(e + par, par)

        @block.tensor
        def _(pe):
            pe.wait_ge(s_tokw, 16)
            pe.wait_ge(s_patch, 32)
            for g in range(4):
                for k in range(PK):
                    mm = pe.matmul(bank[g][:, 0:D], patch_sb[:, k, g * P:(g + 1) * P], tokw_sb[:, k, :],
                                   start=(k == 0), stop=(k == PK - 1))
                mm.then_inc(s_pe_tok, 1)
            pe.wait_ge(s_const, 16 * 5)
            pe.wait_ge(s_wqkv, 32)
            pe.wait_ge(s_wo, 64)
            pe.wait_ge(s_ones, 1)
            pe.wait_ge(s_ptok, 4)

            def iteration(i, i0, par, a, b, c, d):
                if a:
                    pe.wait_ge(s_xn, i + 1)
                    if i0 >= 1:
                        pe.wait_ge(s_rope, i)
                    pe.transpose(bank[4][:, 0:P], xn[:, 0:D0], ident_sb[:, :])
                    pe.transpose(bank[4][0:D1, P:2 * P], xn[:, D0:D], ident_sb[:, :]).then_inc(s_xt, 1)
                if b:
                    pe.wait_ge(s_qkT, 2 * i)
                    if i0 >= 2:
                        pe.wait_ge(s_pT, 2 * (i - 1))
                    q = 1 - par
                    for j in range(4):
                        for g in range(HG):
                            for lo in (0, HALF):
                                mm = pe.matmul(bank[j][lo:lo + HALF, g * S:(g + 1) * S],
                                               qkT[32 * j:32 * j + HD, q, 0, g, lo:lo + HALF],
                                               qkT[32 * j:32 * j + HD, q, 1, g, lo:lo + S],
                                               start=True, stop=True)
                    mm.then_inc(s_sc, 1)
                if c:
                    pe.wait_ge(s_pT, 2 * (i - 1))
                    pe.wait_ge(s_v, 4 * (i - 1))
                    if i0 >= 3:
                        pe.wait_ge(s_x2, i - 2)
                    for p in range(HEADS // 2):
                        for two in range(2):
                            lo = two * HALF
                            w = 2 * (HD + 1)
                            mm = pe.matmul(bank[6][lo:lo + HALF, p * w:(p + 1) * w],
                                           pT[:, par, p, lo:lo + HALF],
                                           vbd[:, par, two, p, :, :].rearrange("p a b -> p (a b)"),
                                           start=True, stop=True)
                    mm.then_inc(s_pv, 1)
                if d:
                    pe.wait_ge(s_x2, i - 2)
                    if i0 >= 4:
                        pe.wait_ge(s_slot, i - 3)
                    pe.transpose(bank[7][:, 0:P], x2[:, 1 - par, 0:D0], ident_sb[:, :])
                    pe.transpose(bank[7][0:D1, P:2 * P], x2[:, 1 - par, D0:D], ident_sb[:, :]).then_inc(s_x2t, 1)
                if a:
                    pe.wait_ge(s_xT, i + 1)
                    x0 = xT0[:, :, :, :].rearrange("p a b c -> p (a b c)")
                    x1 = xT1[:, :, :, :].rearrange("p a b c -> p (a b c)")
                    pe.matmul(bank[4][:, 0:2 * D], x0[:, HALF:3 * HALF], wqkv0_sb[:, 0:2 * D], start=True, stop=False)
                    pe.matmul(bank[4][:, 0:2 * D], x1[:, HALF:3 * HALF], wqkv1_sb[:, 0:2 * D], start=False, stop=True)
                    if i0 >= 1:
                        pe.wait_ge(s_v, 4 * i)
                    for two in range(2):
                        o = bank[5][:, two * D:(two + 1) * D]
                        pe.matmul(o, x0[:, two * P:(two + 1) * P], wqkv0_sb[:, 2 * D:3 * D], start=True, stop=False)
                        mm = pe.matmul(o, x1[:, two * P:(two + 1) * P], wqkv1_sb[:, 2 * D:3 * D], start=False, stop=True)
                    mm.then_inc(s_qkv, 1)
                if c:
                    pe.wait_ge(s_att, i - 1)
                    pe.transpose(bank[6][:, 0:P], att[:, 0:D0], ident_sb[:, :])
                    pe.transpose(bank[6][0:D1, P:2 * P], att[:, D0:D], ident_sb[:, :]).then_inc(s_ot, 1)
                if d:
                    pe.wait_ge(s_x2T, i - 2)
                    pe.matmul(bank[7][:, 0:E], x2T0[:, :], gate_sb[:, 0, :], start=True, stop=False)
                    pe.matmul(bank[7][:, 0:E], x2T1[:, :], gate_sb[0:D1, 1, :], start=False, stop=True).then_inc(s_gate, 1)
                if b:
                    pe.wait_ge(s_exp, i)
                    for p in range(HEADS // 2):
                        mm = pe.transpose(bank[p // 3][:, (p % 3) * P:(p % 3 + 1) * P],
                                          pr[:, 2 * p:2 * p + 2, :].rearrange("p a b -> p (a b)"), ident_sb[:, :])
                        if p % 3 == 2:
                            mm.then_inc(s_pt, 1)
                if c:
                    pe.wait_ge(s_oT, i - 1)
                    pe.matmul(bank[6][:, 0:D], oT0[:, :], wo0_sb[:, :], start=True, stop=False)
                    pe.matmul(bank[6][:, 0:D], oT1[:, :], wo1_sb[:, :], start=False, stop=True).then_inc(s_proj, 1)
                if d:
                    pe.wait_ge(s_hots, i - 2)
                    pe.matmul(bank[7][:, 0:E], order_sb[:, 0:P], hots[:, :], start=True, stop=True)
                    pe.matmul(bank[7][:, E:2 * E], order_sb[:, P:2 * P], hots[:, :], start=True, stop=True).then_inc(s_pos, 1)
                if a:
                    pe.wait_ge(s_qk, i + 1)
                    if b:
                        pe.wait_ge(s_scread, i)
                    for r in range(2):
                        for g in range(HG):
                            mm = pe.transpose(bank[2 + r][:, g * P:(g + 1) * P],
                                              qk[:, r, 4 * g:4 * g + 4, :].rearrange("p a b -> p (a b)"), ident_sb[:, :])
                        mm.then_inc(s_qkt, 1)

            pipeline(pe, iteration)

            def turn(e, par):
                pe.wait_ge(s_zn, CC * (e + 1))
                for c in range(CC):
                    pe.transpose(bank[4][:, c * CR:(c + 1) * CR], zn[:, c, 0:D0], ident_sb[0:CR, 0:CR])
                    mm = pe.transpose(bank[5][0:D1, c * CR:(c + 1) * CR], zn[:, c, D0:D], ident_sb[0:CR, 0:CR])
                mm.then_inc(s_zt, 1)

            def expert(e, e0, par, more):
                pe.wait_ge(s_w[par], 24 * (e - par) + 48)
                pe.wait_ge(s_z, 2 * (e + 1))
                for m in range(MH):
                    q = 2 * (m % 2)
                    if e0 >= 1 or m >= 2:
                        pe.wait_ge(s_hT, MH * e + m - 1)
                    for r in range(2):
                        cols = slice(r * H + m * P, r * H + (m + 1) * P)
                        pe.matmul(bank[q + r][:, 0:CAP], w13a_sb[:, par, cols], z0[:, par, :], start=True, stop=False)
                        mm = pe.matmul(bank[q + r][:, 0:CAP], w13b_sb[:, par, cols], z1[:, par, :], start=False, stop=True)
                    mm.then_inc(s_up, 1)
                if more:
                    turn(e + 1, 1 - par)
                pe.wait_ge(s_hT, MH * (e + 1))
                for c in range(CC):
                    if c % 2 == 0 and e0 >= 1:
                        pe.wait_ge(s_yx, 2 * e + (c // 2 - 1))
                    for m in range(MH):
                        mm = pe.matmul(bank[6 + c // 2][0:CR, (c % 2) * D:(c % 2 + 1) * D],
                                       hT[:, m, c * CR:(c + 1) * CR], w2_sb[:, par, m, :],
                                       start=(m == 0), stop=(m == MH - 1))
                    if c % 2 == 1:
                        mm.then_inc(s_down, 1)

            turn(0, 0)
            expert(0, 0, 0, True)
            expert(1, 1, 1, True)
            with pe.Fori(1, E // 2 - 1) as pair:
                expert(pair * 2, 2, 0, True)
                expert(pair * 2 + 1, 3, 1, True)
            expert(E - 2, E - 2, 0, True)
            expert(E - 1, E - 1, 1, False)

        @block.scalar
        def _(act):
            act.wait_ge(s_ones, 1)

            def iteration(i, i0, par, a, b, c, d):
                if a:
                    act.wait_ge(s_xt, i + 1)
                    if i0 >= 1:
                        act.wait_ge(s_qkv, i)
                    for n, xT, at in ((P, xT0, 0), (D1, xT1, P)):
                        turned = bank[4][0:n, at:at + P].rearrange("p (a c) -> p a c", a=2)
                        ins = act.copy(xT[0:n, :, :, :], turned.unsqueeze(2).to_broadcast([n, 2, 2, HALF]))
                    ins.then_inc(s_xT, 1)
                if d:
                    act.wait_ge(s_x2t, i - 2)
                    if i0 >= 4:
                        act.wait_ge(s_gate, i - 3)
                    act.copy(x2T0[:, :], bank[7][:, 0:P])
                    act.copy(x2T1[:, :], bank[7][0:D1, P:2 * P]).then_inc(s_x2T, 1)
                    if i0 >= 4:
                        act.wait_ge(s_ms, i - 3)
                    act.activation(squares[:, :], x2[:, 1 - par, :], ACT.Square, scale=2.0 * D ** -0.5,
                                   accum_out=ssq[:, :]).then_inc(s_ssq, 1)
                    if i0 >= 5:
                        act.wait_ge(s_disp[1 - par], 16 * (i - 3 - (1 - par)))
                    act.copy(row[:, 1 - par, :, 0:D],
                             x2[:, 1 - par, :].unsqueeze(1).to_broadcast([P, 2, D])).then_inc(s_rowx, 1)
                if c:
                    act.wait_ge(s_ot, i - 1)
                    if i0 >= 3:
                        act.wait_ge(s_proj, i - 2)
                    act.copy(oT0[:, :], bank[6][:, 0:P])
                    act.copy(oT1[0:D1, :], bank[6][0:D1, P:2 * P]).then_inc(s_oT, 1)
                if b:
                    act.wait_ge(s_sh, i)
                    if i0 >= 2:
                        act.wait_ge(s_pt, 2 * (i - 1))
                    act.activation(pr[:, :, 0:S].rearrange("p (g j) k -> p j g k", j=4),
                                   sm[:, :].rearrange("p (j g k) -> p j g k", j=4, g=HG), ACT.Exp).then_inc(s_exp, 1)
                if a:
                    act.wait_ge(s_qkv, i + 1)
                    if i0 >= 2:
                        act.wait_ge(s_pv, i - 1)
                    for two in range(2):
                        for odd in range(2):
                            lo = odd * HALF
                            act.copy(vbd[lo:lo + HALF, par, two, :, odd, 0:HD],
                                     bank[5][lo:lo + HALF, two * D:(two + 1) * D].rearrange(
                                         "p (a b d) -> p a b d", b=2, d=HD)[:, :, odd, :]).then_inc(s_v, 1)
                if b:
                    for r in range(2):
                        act.wait_ge(s_pt, 2 * (i - 1) + r + 1)
                        if r == 0 and i0 >= 3:
                            act.wait_ge(s_pv, i - 2)
                        act.copy(pT[:, 1 - par, 3 * r:3 * r + 3, :].rearrange("p a b -> p (a b)"),
                                 bank[r][:, 0:3 * P]).then_inc(s_pT, 1)
                if d:
                    act.wait_ge(s_diff, i - 2)
                    if i0 >= 4:
                        act.wait_ge(s_slot, i - 3)
                    act.activation(ratio[:, :], gapd[:, :], ACT.Exp).then_inc(s_ratio, 1)
                if a:
                    for r in range(2):
                        act.wait_ge(s_qkt, 2 * i + r + 1)
                        if r == 0 and (i0 >= 2):
                            act.wait_ge(s_sc, i - 1)
                        act.copy(qkT[:, par, r, :, :].rearrange("p a b -> p (a b)"),
                                 bank[2 + r][:, 0:3 * P]).then_inc(s_qkT, 1)

            pipeline(act, iteration)

            def prepare(e, e0, par):
                act.wait_ge(s_zt, e + 1)
                if e0 >= 2:
                    act.wait_ge(s_up, MH * (e - 1))
                idx = e
                act.mul(z0[:, par, :], bank[4][:, 0:CAP], nw0_sb[:, bass.ds(idx, 1)]).then_inc(s_z, 1)
                act.mul(z1[:, par, :], bank[5][0:D1, 0:CAP], nw1_sb[:, bass.ds(idx, 1)]).then_inc(s_z, 1)

            def expert(e, e0, par, more):
                for m in range(MH):
                    act.wait_ge(s_up, MH * e + m + 1)
                    if e0 >= 1 or m >= 2:
                        act.wait_ge(s_hT, MH * e + m - 1)
                    act.activation(sg[:, m % 2, :], bank[2 * (m % 2)][:, 0:CAP], ACT.Silu).then_inc(s_silu, 1)
                if more:
                    prepare(e + 1, e0 + 1, 1 - par)
                for c in range(CC):
                    act.wait_ge(s_yx, 2 * e + c // 2 + 1)
                    if e0 >= 1 and c == 0:
                        act.wait_ge(s_add, 64 * e)
                    act.mul(yw[:, c, :], yx[:, c, :], zs[:, par, c, W_COL:W_COL + 1]).then_inc(s_yw, 1)

            act.wait_ge(s_nw, 32)
            prepare(0, 0, 0)
            expert(0, 0, 0, True)
            expert(1, 1, 1, True)
            with act.Fori(1, E // 2 - 1) as pair:
                expert(pair * 2, 2, 0, True)
                expert(pair * 2 + 1, 3, 1, True)
            expert(E - 2, E - 2, 0, True)
            expert(E - 1, E - 1, 1, False)

        @block.vector
        def _(dve):
            dve.memset(zero_sb[:, :, :], 0.0).then_inc(s_pre, 1)
            dve.wait_ge(s_pre, 1)
            dve.memset(xT1[D1:D1 + 1, :, :, :], 1.0)
            dve.memset(oT1[D1:D1 + 1, :], 1.0)
            dve.memset(qk[:, :, :, :], 0.0)
            dve.memset(pr[:, :, :], 0.0)
            dve.memset(count[:, :], 0.0)
            dve.memset(row[:, :, :, ROW - 1:ROW], 0.0)
            dve.memset(vbd[:, :, :, :, :, :], 0.0).then_inc(s_pre, 1)
            dve.wait_ge(s_pre, 2)
            dve.memset(vbd[0:HALF, :, :, :, 0, HD:HD + 1], 1.0)
            dve.memset(vbd[HALF:P, :, :, :, 1, HD:HD + 1], 1.0).then_inc(s_ones, 1)
            dve.wait_ge(s_posb, 32)
            dve.tensor_tensor(posb_sb[:, :], posb_sb[:, :], tokb_sb[:, :], ALU.add).then_inc(s_posum, 1)
            dve.wait_ge(s_posum, 1)
            for g in range(4):
                dve.wait_ge(s_pe_tok, g + 1)
                dve.tensor_tensor(ptok_sb[:, g, :], bank[g][:, 0:D], posb_sb[:, :], ALU.add).then_inc(s_ptok, 1)
            dve.wait_ge(s_const, 16 * 5)
            dve.tensor_copy(zero_sb[:, :, ID_COL], small_sb[:, SPARE0:SPARE0 + SPP]).then_inc(s_zero, 1)
            dve.tensor_copy(order_sb[:, :], orderf_sb[:, :]).then_inc(s_order, 1)
            dve.wait_ge(s_gaps, 1)
            dve.wait_ge(s_txt, 32)
            dve.wait_ge(s_ptok_in, 32)
            for t in range(NT):
                ins = dve.bn_stats(stats[:, t, :], h_all[:, t, :])
            ins.then_inc(s_pre, 1)
            dve.wait_ge(s_pre, 3)
            for t in range(NT):
                ins = dve.bn_aggr(mv[:, t, :], stats[:, t, :])
            ins.then_inc(s_pre, 1)
            dve.wait_ge(s_pre, 4)
            dve.tensor_scalar(ve1[:, :], mv[:, :, 1], LN_EPS, None, ALU.add).then_inc(s_stat, 1)
            dve.wait_ge(s_rstd1, 1)

            def norm1(t, t0):
                if t0 >= 1:
                    dve.wait_ge(s_xt, t)
                dve.tensor_scalar(xn[:, :], h_all[:, bass.ds(t, 1), :].rearrange("p a d -> p (a d)"),
                                  mv[:, bass.ds(t, 1), 0], rstd1[:, bass.ds(t, 1)],
                                  ALU.subtract, ALU.mult).then_inc(s_xn, 1)

            def steps(sem_, name, t):
                k = [0]

                def link(ins, wait=True):
                    k[0] += 1
                    ins.then_inc(sem_, 1)
                    if wait:
                        dve.wait_ge(sem_, STEPS[name] * t + k[0])

                def done():
                    assert k[0] == STEPS[name], (name, k[0])
                return link, done

            norm1(0, 0)

            def iteration(i, i0, par, a, b, c, d):
                if b:
                    linkb, doneb = steps(sB, "B", i - 1)
                    dve.wait_ge(s_sc, i)
                    if i0 >= 2:
                        dve.wait_ge(s_exp, i - 1)
                    for j in range(4):
                        ins = dve.tensor_tensor(sm[:, j * HG * S:(j + 1) * HG * S], bank[j][:, 0:HG * S],
                                                mask_sb[:, 0:HG, :].rearrange("p a b -> p (a b)"), ALU.add)
                        if j == 3:
                            ins.then_inc(s_scread, 1)
                    dve.wait_ge(s_scread, i)
                    sm3 = sm[:, :].rearrange("p (h k) -> p h k", k=S)
                    linkb(dve.tensor_reduce(mx[:, :], sm3, AX.X, ALU.max))
                    dve.tensor_tensor(sm3, sm3, mx[:, :].unsqueeze(2).to_broadcast([P, HEADS, S]),
                                      ALU.subtract).then_inc(s_sh, 1)
                    doneb()
                if c:
                    link, done = steps(sC, "C", i - 2)
                    dve.wait_ge(s_pv, i - 1)
                    o4 = bank[6][:, 0:HEADS * (HD + 1)].rearrange("p (h d) -> p h d", h=HEADS)
                    link(dve.reciprocal(rden[:, :], o4[:, :, HD]))
                    if i0 >= 3:
                        dve.wait_ge(s_ot, i - 2)
                    dve.tensor_tensor(att[:, :].rearrange("p (h d) -> p h d", h=HEADS), o4[:, :, 0:HD],
                                      rden[:, :].unsqueeze(2).to_broadcast([P, HEADS, HD]),
                                      ALU.mult).then_inc(s_att, 1)
                if a:
                    dve.wait_ge(s_qkv, i + 1)
                    if i0 >= 1:
                        dve.wait_ge(s_qk, i)
                    q2 = bank[4][:, 0:2 * D]
                    dve.tensor_tensor(rc[:, :], q2, rope_sb[:, 0, :], ALU.mult)
                    pairs = q2.rearrange("p (n two) -> p n two", two=2)
                    rs2 = rs[:, :].rearrange("p (n two) -> p n two", two=2)
                    sn2 = rope_sb[:, 1, :].rearrange("p (n two) -> p n two", two=2)
                    dve.tensor_tensor(rs2[:, :, 0], pairs[:, :, 1], sn2[:, :, 0], ALU.mult)
                    dve.tensor_tensor(rs2[:, :, 1], pairs[:, :, 0], sn2[:, :, 1], ALU.mult).then_inc(s_rope, 1)
                rev = small_sb[:, REV0:REV0 + E]
                if c:
                    dve.wait_ge(s_proj, i - 1)
                    ht = h_all[:, bass.ds(i - 2, 1), :].rearrange("p a d -> p (a d)")
                    link(dve.tensor_tensor(ht, bank[6][:, 0:D], ht, ALU.add))
                if a and i0 + 1 < NT:
                    norm1(i + 1, i0 + 1)
                if c:
                    link(dve.bn_stats(st2[:, :], ht))
                if d:
                    linkd, doned = steps(sD, "D", i - 3)
                    dve.wait_ge(s_gate, i - 2)
                    linkd(dve.tensor_copy(lg[:, :], bank[7][:, 0:E]), wait=False)
                if c:
                    link(dve.bn_aggr(mv2[:, :], st2[:, :]))
                    if i0 >= 3:
                        dve.wait_ge(s_rstd2, i - 2)
                    dve.tensor_scalar(ve2[:, :], mv2[:, 1:2], LN_EPS, None, ALU.add).then_inc(s_var2, 1)
                    done()
                if d:
                    t = i - 3
                    dve.wait_ge(sD, STEPS["D"] * t + 1)
                    linkd(dve.tensor_reduce(top[:, 0:1], lg[:, :], AX.X, ALU.max))
                    linkd(dve.scalar_tensor_tensor(cand[:, 0, :], lg[:, :], top[:, 0:1], rev, ALU.is_ge, ALU.mult))
                    linkd(dve.tensor_reduce(rank[:, 0:1], cand[:, 0, :], AX.X, ALU.max))
                    linkd(dve.tensor_scalar(hot[:, 0, :], rev, rank[:, 0:1], None, ALU.is_equal))
                    linkd(dve.scalar_tensor_tensor(lg2[:, :], hot[:, 0, :], -1.0e30, lg[:, :], ALU.mult, ALU.add))
                    linkd(dve.tensor_reduce(top[:, 1:2], lg2[:, :], AX.X, ALU.max))
                    if i0 >= 4:
                        dve.wait_ge(s_ratio, i - 3)
                    dve.tensor_tensor(gapd[:, :], top[:, 1:2], top[:, 0:1], ALU.subtract).then_inc(s_diff, 1)
                    linkd(dve.scalar_tensor_tensor(cand[:, 1, :], lg2[:, :], top[:, 1:2], rev, ALU.is_ge, ALU.mult))
                    linkd(dve.tensor_reduce(rank[:, 1:2], cand[:, 1, :], AX.X, ALU.max))
                    linkd(dve.tensor_scalar(hot[:, 1, :], rev, rank[:, 1:2], None, ALU.is_equal))
                    dve.tensor_tensor(hots[:, :], hot[:, 0, :], hot[:, 1, :], ALU.add).then_inc(s_hots, 1)
                    linkd(dve.tensor_scalar(base[:, :], rank[:, :], -float(CAP), float(CAP * E), ALU.mult, ALU.add))
                    dve.wait_ge(s_ratio, i - 2)
                    linkd(dve.tensor_scalar(total[:, :], ratio[:, :], 1.0, None, ALU.add))
                    linkd(dve.reciprocal(wts[:, 0:1], total[:, :]))
                    linkd(dve.tensor_tensor(wts[:, 1:2], wts[:, 0:1], ratio[:, :], ALU.mult))
                if c:
                    dve.wait_ge(s_rstd2, i - 1)
                    if i0 >= 4:
                        dve.wait_ge(s_rowx, i - 3)
                        dve.wait_ge(s_x2t, i - 3)
                        dve.wait_ge(s_ssq, i - 3)
                    dve.tensor_scalar(x2[:, par, :], ht, mv2[:, 0:1], rstd2[:, :], ALU.subtract,
                                      ALU.mult).then_inc(s_x2, 1)
                if d:
                    dve.wait_ge(s_pos, i - 2)
                    linkd(dve.tensor_tensor(pos[:, :], bank[7][:, 0:E], count[:, :], ALU.add))
                    linkd(dve.tensor_tensor(count[:, :], bank[7][:, E:2 * E], count[:, :], ALU.add))
                    linkd(dve.tensor_tensor(posk[:, :, :], hot[:, :, :],
                                            pos[:, :].unsqueeze(1).to_broadcast([P, 2, E]), ALU.mult))
                    linkd(dve.tensor_reduce(pk[:, :], posk[:, :, :], AX.X, ALU.add))
                    linkd(dve.tensor_scalar(over[:, :], pk[:, :], float(CAP), FAR, ALU.is_ge, ALU.mult))
                    linkd(dve.tensor_scalar(keep[:, :], pk[:, :], float(CAP), None, ALU.is_lt))
                    linkd(dve.tensor_tensor(base[:, :], base[:, :], pk[:, :], ALU.add))
                    q = 1 - par
                    if i0 >= 5:
                        dve.wait_ge(s_disp[q], 16 * (t - q))
                    linkd(dve.tensor_tensor(row[:, q, :, W_COL], wts[:, :], keep[:, :], ALU.mult))
                    dve.scalar_tensor_tensor(slot[:, q, :], over[:, :], small_sb[:, GAP0:GAP0 + 1], base[:, :],
                                             ALU.add, ALU.add).then_inc(s_slot, 1)
                    doned()

            pipeline(dve, iteration)

            def scale(e, e0, par):
                dve.wait_ge(s_zs[par], 8 * (e - par) + 16)
                if e0 >= 1:
                    dve.wait_ge(s_zt, e)
                if e0 >= 2:
                    dve.wait_ge(s_add, 64 * (e - 1))
                dve.tensor_copy(tok[:, par, :], zs[:, par, :, ID_COL]).then_inc(s_tok, 1)
                for c in range(CC):
                    dve.tensor_scalar(zn[:, c, :], zs[:, par, c, 0:D], zs[:, par, c, RMS_COL:RMS_COL + 1],
                                      None, ALU.mult).then_inc(s_zn, 1)

            def expert(e, e0, par, more):
                if more:
                    scale(e + 1, e0 + 1, 1 - par)
                for m in range(MH):
                    dve.wait_ge(s_silu, MH * e + m + 1)
                    if e0 >= 1 and m == 0:
                        dve.wait_ge(s_down, 2 * e)
                    dve.tensor_tensor(hT[:, m, :], sg[:, m % 2, :], bank[2 * (m % 2) + 1][:, 0:CAP],
                                      ALU.mult).then_inc(s_hT, 1)
                for r in range(2):
                    dve.wait_ge(s_down, 2 * e + r + 1)
                    if e0 >= 1 and r == 0:
                        dve.wait_ge(s_yw, CC * e)
                    dve.tensor_tensor(yx[:, 2 * r:2 * r + 2, :],
                                      bank[6 + r][0:CR, 0:2 * D].rearrange("p (a d) -> p a d", a=2),
                                      zs[:, par, 2 * r:2 * r + 2, 0:D], ALU.add).then_inc(s_yx, 1)

            scale(0, 0, 0)
            expert(0, 0, 0, True)
            expert(1, 1, 1, True)
            with dve.Fori(1, E // 2 - 1) as pair:
                expert(pair * 2, 2, 0, True)
                expert(pair * 2 + 1, 3, 1, True)
            expert(E - 2, E - 2, 0, True)
            expert(E - 1, E - 1, 1, False)

        @block.gpsimd
        def _(pool):
            pool.memset(h_all[32:64, :, :], 0.0)
            pool.memset(h_all[96:P, :, :], 0.0).then_inc(s_gaps, 1)
            pool.wait_ge(s_const, 16 * 5)
            pool.wait_ge(s_stat, 1)
            pool.tensor_tensor(rstd1[:, :], ve1[:, :], small_sb[:, POW0:POW0 + NT], ALU.pow).then_inc(s_rstd1, 1)
            pool.wait_ge(s_slots0, 16)

            def iteration(i, i0, par, a, b, c, d):
                t, q = i - 3, 1 - par
                if d:
                    pool.wait_ge(s_ssq, i - 2)
                    pool.tensor_tensor(ms[:, :], ssq[:, :], small_sb[:, EPS0:EPS0 + 1], ALU.add).then_inc(s_ms, 1)
                    pool.wait_ge(s_ms, i - 2)
                    pool.tensor_tensor(rms[:, :], ms[:, :], small_sb[:, POW0:POW0 + 1], ALU.pow).then_inc(s_rms, 1)
                    if i0 >= 5:
                        pool.wait_ge(s_disp[q], 16 * (t - q))
                    pool.wait_ge(s_rms, i - 2)
                    pool.tensor_tensor(row[:, q, :, RMS_COL], rms[:, :].to_broadcast([P, 2]),
                                       small_sb[:, TWO0:TWO0 + 2], ALU.mult)
                    pool.tensor_copy(row[:, q, :, ID_COL],
                                     small_sb[:, bass.ds(t + IDS0, 1)].to_broadcast([P, 2])).then_inc(s_rowid, 1)
                if a:
                    pool.wait_ge(s_rope, i + 1)
                    if i0 >= 1:
                        pool.wait_ge(s_qkt, 2 * i)
                    pool.tensor_tensor(qk[:, :, :, 0:HD].rearrange("p a h d -> p (a h) d"),
                                       rc[:, :].rearrange("p (h d) -> p h d", d=HD),
                                       rs[:, :].rearrange("p (h d) -> p h d", d=HD), ALU.add).then_inc(s_qk, 1)
                if c:
                    pool.wait_ge(s_var2, i - 1)
                    if i0 >= 3:
                        pool.wait_ge(s_x2, i - 2)
                    pool.tensor_tensor(rstd2[:, :], ve2[:, :], small_sb[:, POW0:POW0 + 1],
                                       ALU.pow).then_inc(s_rstd2, 1)
                if d:
                    pool.wait_ge(s_ones, 1)
                    pool.wait_ge(s_rowid, i - 2)
                    pool.wait_ge(s_rowx, i - 2)
                    pool.wait_ge(s_slot, i - 2)
                    for k in range(2):
                        pool.indirect_dma_start(
                            out=slots, out_offset=bass.IndirectOffsetOnAxis(ap=slot[:, q, k:k + 1], axis=0),
                            in_=row[:, q, k, :], in_offset=None,
                            bounds_check=E * CAP - 1, oob_is_err=False).then_inc(s_disp[q], 16)

            pipeline(pool, iteration)

            pool.wait_ge(s_h_out, 48)
            for e in range(E):
                pool.wait_ge(s_tok, e + 1)
                if e >= 1:
                    pool.wait_ge(s_add, 64 * e)
                for c in range(CC):
                    pool.wait_ge(s_yw, CC * e + c + 1)
                    pool.indirect_dma_start(
                        out=out, out_offset=bass.IndirectOffsetOnAxis(ap=tok[:, e % 2, c:c + 1], axis=0),
                        in_=yw[:, c, :], in_offset=None,
                        bounds_check=N + CAP - 1, oob_is_err=True, compute_op=ALU.add).then_inc(s_add, 16)
            pool.wait_ge(s_add, 64 * E)


_INS = ["patches", "txt", "posb", "tokb", "tokw", "wqkv", "wo", "gate", "w13", "w2", "normw",
        "rope", "mask", "small", "order", "ident"]


def kernel(x, txt, L0_tok_W, L0_tok_b, L0_tok_pos_emb, L0_attn_Wq, L0_attn_bq, L0_attn_Wk, L0_attn_bk,
           L0_attn_Wv, L0_attn_bv, L0_attn_Wo, L0_attn_bo, L0_ffn_gate_w, L0_ffn_w13, L0_ffn_w2,
           L0_ffn_norm_w):
    import concourse.bacc as bacc
    from concourse.bass_utils import run_bass_kernel_spmd

    g = IMG // PATCH
    a = {k: np.asarray(v) for k, v in locals().copy().items() if isinstance(v, np.ndarray) or hasattr(v, "dtype")}
    flat = a["x"].reshape(B, g, PATCH, g, PATCH, CH).transpose(2, 4, 5, 0, 1, 3).reshape(PK, P, B * NPATCH)
    arrays = {
        "patches": flat.transpose(1, 0, 2),
        "txt": a["txt"],
        "posb": np.tile(a["L0_tok_pos_emb"], (P // NPATCH, 1)),
        "tokb": np.tile(a["L0_tok_b"][None, :], (P, 1)),
        "tokw": a["L0_tok_W"].reshape(PK, P, D).transpose(1, 0, 2),
        "wqkv": np.concatenate([
            np.concatenate([a["L0_attn_Wq"], a["L0_attn_Wk"], a["L0_attn_Wv"]], axis=1),
            np.concatenate([a["L0_attn_bq"], a["L0_attn_bk"], a["L0_attn_bv"]])[None, :]], axis=0),
        "wo": np.concatenate([a["L0_attn_Wo"], a["L0_attn_bo"][None, :]], axis=0),
        "gate": a["L0_ffn_gate_w"].T,
        "w13": a["L0_ffn_w13"].transpose(0, 2, 1).reshape(E * D, 2 * H),
        "w2": a["L0_ffn_w2"].transpose(0, 2, 1).reshape(E * H, D),
        "normw": a["L0_ffn_norm_w"].T,
        **shape_constants(),
    }
    nc = bacc.Bacc("TRN2", target_bir_lowering=False, num_devices=1)
    feeds, args = {}, []
    for name in _INS:
        arr = np.ascontiguousarray(arrays[name])
        feeds[f"in_{name}"] = arr
        args.append(nc.dram_tensor(f"in_{name}", arr.shape, mybir.dt.from_np(arr.dtype), kind="ExternalInput").ap())
    args.append(nc.dram_tensor("out_rows", (N + CAP, D), F32, kind="ExternalOutput").ap())
    build(nc, *args)
    got = run_bass_kernel_spmd(nc, [feeds], core_ids=[0]).results[0]["out_rows"]
    return got[:N].reshape(B, S, D)
```

```python
from contextlib import ExitStack

import numpy as np

import concourse.bass as bass
from concourse import mybir

F32 = mybir.dt.float32
F32R = mybir.dt.float32r
BF16 = mybir.dt.bfloat16
U32 = mybir.dt.uint32
ALU = mybir.AluOpType
ACT = mybir.ActivationFunctionType
AX = mybir.AxisListType

P = 128
B, IMG, PATCH, CH = 32, 64, 16, 3
NPATCH = (IMG // PATCH) ** 2
PDIM = PATCH * PATCH * CH
PK = PDIM // P
NTXT = 32
S = NPATCH + NTXT
D = 192
D0, D1 = P, D - P
HEADS, HD = 12, 16
HG = HEADS // 4
NT = B // 2
HALF = 64
N = B * S
E, H = 8, 512
MH = H // P
CAP = -(-5 * 2 * N // (4 * E))
CC, CR = 4, CAP // 4
ROW = D + E + 2
W_COL, ID_COL, RMS_COL = D, D + E, D + E + 1
SPP = E * CAP // P
FAR = 1.0e5
LN_EPS, RMS_EPS = 1e-5, 1e-6
assert CAP == 480 and N == 1536


def shape_constants():
    c = {}
    half = D // 2
    inv = (1.0 / np.float32(10000.0) ** (np.arange(half, dtype=np.float32) * np.float32(2.0) / np.float32(D))).astype(np.float32)
    ang = (np.arange(S, dtype=np.float32)[:, None] * inv[None, :]).astype(np.float32)
    cos, sin = np.cos(ang), np.sin(ang)
    cos2 = np.repeat(cos, 2, axis=1)
    sin2 = np.stack([-sin, sin], axis=-1).reshape(S, D)
    rope = np.zeros((P, 2, 2, D), np.float32)
    mask = np.zeros((P, S), np.float32)
    causal = np.where(np.tril(np.ones((S, S), bool)), 0.0, -1.0e30).astype(np.float32)
    for lo in (0, HALF):
        for j, scale in ((0, HD ** -0.5), (1, 1.0)):
            rope[lo:lo + S, 0, j] = cos2 * scale
            rope[lo:lo + S, 1, j] = sin2 * scale
        mask[lo:lo + S] = causal
    c["rope"] = rope.reshape(P, -1)
    c["mask"] = np.tile(mask, (1, HEADS))
    live = np.zeros(P, bool)
    live[:S] = live[HALF:HALF + S] = True
    experts = np.tile(np.arange(E, dtype=np.float32), (P, 1))
    gap = np.where(live, 0.0, FAR).astype(np.float32)[:, None]
    ids = np.full((P, NT), FAR, np.float32)
    for t in range(NT):
        ids[0:S, t] = (2 * t) * S + np.arange(S)
        ids[HALF:HALF + S, t] = (2 * t + 1) * S + np.arange(S)
    power = np.full((P, NT), -0.5, np.float32)
    power = np.concatenate([power, np.full((P, 2), RMS_EPS / 4, np.float32)], axis=1)
    spare = (N + np.arange(E * CAP) % CAP).reshape(P, SPP).astype(np.float32)
    c["small"] = np.concatenate([experts, gap, power, ids, spare], axis=1)
    before = (np.arange(P)[:, None] < np.arange(P)[None, :]) & live[:, None]
    every = np.repeat(live[:, None], P, axis=1)
    c["order"] = np.concatenate([before, every], axis=1).astype(np.float32)
    c["ident"] = np.eye(P, dtype=np.float32)
    return c


EXP0, GAP0, POW0 = 0, E, E + 1
EPS0 = POW0 + NT
IDS0 = EPS0 + 2
SPARE0 = IDS0 + NT
SMALL = SPARE0 + SPP

PEEL = 6

STEPS = {"B": 1, "C": 1, "R1": 3, "R2": 8}


def build(nc, patches, txt, posb, tokb, tokw, wqkv, wo, gate, w13, w2, normw,
          rope, mask, small, order, ident, out):
    slots = nc.dram_tensor("slots", (E * CAP, ROW), F32, kind="Internal").ap()
    fused = nc.dram_tensor("patch_tokens", (B * NPATCH, D), F32, kind="Internal").ap()
    with ExitStack() as ctx:
        def sb(name, shape, dt=F32):
            return ctx.enter_context(nc.sbuf_tensor(name, shape, dt))

        def sem(name):
            return ctx.enter_context(nc.semaphore(name))

        ident_sb = sb("ident_sb", [P, P])
        rope_sb = sb("rope_sb", [P, 2, 2 * D])
        mask_sb = sb("mask_sb", [P, HEADS, S])
        small_sb = sb("small_sb", [P, SMALL])
        orderf_sb = sb("orderf_sb", [P, 2 * P])
        order_sb = sb("order_sb", [P, 2 * P], BF16)
        tokw_sb = sb("tokw_sb", [P, PK, D])
        patch_sb = sb("patch_sb", [P, PK, B * NPATCH])
        posb_sb = sb("posb_sb", [P, D])
        tokb_sb = sb("tokb_sb", [P, D])
        ptok_sb = sb("ptok_sb", [P, 4, D])
        wqkv0_sb = sb("wqkv0_sb", [P, 3 * D])
        wqkv1_sb = sb("wqkv1_sb", [D1 + 1, 3 * D])
        wo0_sb = sb("wo0_sb", [P, D])
        wo1_sb = sb("wo1_sb", [D1 + 1, D])
        gate_sb = sb("gate_sb", [P, 2, E])
        zero_sb = sb("zero_sb", [P, SPP, ROW])
        h_all = sb("h_all", [P, NT, D])
        stats = sb("stats", [P, NT, 6])
        mv = sb("mv", [P, NT, 2])
        ve1 = sb("ve1", [P, NT])
        rstd1 = sb("rstd1", [P, NT])
        xn = sb("xn", [P, D])
        xT0 = sb("xT0", [P, 2, 2, HALF])
        xT1 = sb("xT1", [D1 + 1, 2, 2, HALF])
        rc = sb("rc", [P, 2 * D])
        rs = sb("rs", [P, 2 * D])
        qk = sb("qk", [P, 2, HEADS, 32])
        qT = sb("qT", [P, 2, HG, P])
        kbd = sb("kbd", [P, 2, 2, HG, 4, S])
        vbd = sb("vbd", [P, 2, 2, HEADS // 2, 2, HD + 1])
        sm = sb("sm", [P, HEADS * S])
        mx = sb("mx", [P, HEADS])
        pr = sb("pr", [P, HEADS, 64])
        pT = sb("pT", [P, 2, HEADS // 2, P])
        rden = sb("rden", [P, HEADS])
        att = sb("att", [P, D])
        oT0 = sb("oT0", [P, P])
        oT1 = sb("oT1", [D1 + 1, P])
        st2 = sb("st2", [P, 6])
        mv2 = sb("mv2", [P, 2])
        ve2 = sb("ve2", [P, 1])
        rstd2 = sb("rstd2", [P, 1])
        x2 = sb("x2", [P, 2, D])
        rows = sb("rows", [P, 4, ROW])
        x2T0 = sb("x2T0", [P, P])
        x2T1 = sb("x2T1", [D1, P])
        squares = sb("squares", [P, D])
        ssq = sb("ssq", [P, 2])
        ms = sb("ms", [P, 2])
        lg = sb("lg", [P, E])
        top = sb("top", [P, 2, E])
        choice = sb("choice", [P, 2, E], U32)
        chosen = sb("chosen", [P, 4])
        hot = sb("hot", [P, 2, 2, E])
        hots = sb("hots", [P, 2, E], BF16)
        count = sb("count", [P, E])
        pos = sb("pos", [P, 2, E])
        posk = sb("posk", [P, 2, 2, E])
        pk = sb("pk", [P, 4])
        base = sb("base", [P, 4])
        over = sb("over", [P, 4])
        gapd = sb("gapd", [P, 2])
        ratio = sb("ratio", [P, 2])
        total = sb("total", [P, 2])
        wts = sb("wts", [P, 2, 2])
        wk = sb("wk", [P, 2, 2, E])
        slot = sb("slot", [P, 4], U32)
        rawa_sb = sb("rawa_sb", [P, 2 * H])
        rawb_sb = sb("rawb_sb", [P, 2 * H])
        wah = sb("wah", [P, 2, 2 * H], F32R)
        wal = sb("wal", [P, 2, 2 * H], F32R)
        wbh = sb("wbh", [P, 2, 2 * H], F32R)
        wbl = sb("wbl", [D1, 2, 2 * H], F32R)
        w2_sb = sb("w2_sb", [P, 2, MH, D])
        nw0_sb = sb("nw0_sb", [P, E])
        nw1_sb = sb("nw1_sb", [P, E])
        zs = sb("zs", [CR, 2, CC, ROW])
        zn0 = sb("zn0", [CR, CC, D0])
        zn1 = sb("zn1", [CR, CC, 2, D1])
        z0h = sb("z0h", [P, 2, CAP], F32R)
        z0l = sb("z0l", [P, 2, CAP], F32R)
        z1 = sb("z1", [P, 2, CAP], F32R)
        sg = sb("sg", [P, 2, CAP])
        hT = sb("hT", [P, MH, CAP])
        yx = sb("yx", [CR, CC, D])
        yw = sb("yw", [CR, CC, D])
        tok = sb("tok", [CR, E, CC], U32)

        bank = [ctx.enter_context(nc.psum_tensor(f"bank{i}", [P, 512], F32)) for i in range(8)]

        s_patch = sem("patch_in"); s_tokw = sem("tokw_in"); s_posb = sem("posb_in")
        s_const = sem("const_in"); s_wqkv = sem("wqkv_in"); s_wo = sem("wo_in")
        s_txt = sem("txt_in"); s_ptok_out = sem("patch_tokens_out")
        s_ptok_in = sem("patch_tokens_in"); s_h_out = sem("h_out")
        s_zero = sem("zero_ready"); s_gaps = sem("gaps_ready"); s_ones = sem("ones_ready")
        s_pe_tok = sem("patch_product"); s_posum = sem("pos_bias_sum"); s_ptok = sem("patch_tokens_ready")
        s_order = sem("order_bf16"); s_stat = sem("stats_ready"); s_rstd1 = sem("rstd1_ready")
        s_pre = sem("vector_pre_step")
        s_xn = sem("xn_ready"); s_xt = sem("xn_turned"); s_xT = sem("xT_ready")
        s_qkv = sem("qkv_product"); s_rope = sem("rope_parts"); s_qk = sem("qk_ready")
        s_v = sem("v_ready"); s_qkt = sem("qk_turned"); s_qkT = sem("qkT_ready")
        sA = sem("vector_step_A")
        s_sc = sem("scores"); s_sh = sem("scores_shifted"); s_exp = sem("exp_ready")
        s_pt = sem("probs_turned"); s_pT = sem("pT_ready"); sB = sem("vector_step_B")
        s_scread = sem("scores_read")
        s_pv = sem("values_product"); s_att = sem("attention_ready"); s_ot = sem("attention_turned")
        s_oT = sem("oT_ready"); s_proj = sem("projection"); s_var2 = sem("variance2_ready")
        s_rstd2 = sem("rstd2_ready"); s_x2 = sem("x2_ready"); sC = sem("vector_step_C")
        s_res = sem("residual_added"); s_st2 = sem("statistics2"); s_mv2 = sem("mean_variance2")
        s_x2t = sem("x2_turned"); s_x2T = sem("x2T_ready"); s_ssq = sem("square_sum")
        s_ms = sem("mean_square"); s_rms = sem("rms_ready"); s_gate = sem("logits")
        s_lg = sem("logits_copied"); s_top = sem("logits_sorted"); s_choice = sem("choice_ready")
        s_chosen = sem("chosen_ready"); s_diff = sem("logit_gap"); s_ratio = sem("ratio_ready")
        s_hots = sem("hots_ready"); s_pos = sem("positions"); s_slot = sem("slot_ready")
        s_disp = sem("slots_written"); sR1 = sem("vector_step_R1")
        sR2 = sem("vector_step_R2"); s_rowx = sem("row_x_ready")
        s_raw = sem("w13_in"); s_w2 = [sem("w2_in_even"), sem("w2_in_odd")]; s_nw = sem("norm_w_in")
        s_zs = [sem("slots_in_even"), sem("slots_in_odd")]
        s_zn = sem("z_scaled"); s_zt = sem("z_turned"); s_zh = sem("z_high"); s_z = sem("z_ready")
        s_wh = sem("weights_high"); s_wl = sem("weights_rest")
        s_up = sem("up_product"); s_silu = sem("silu_ready"); s_hT = sem("hidden_ready")
        s_down = sem("down_product"); s_yx = sem("y_plus_x"); s_yw = sem("y_weighted")
        s_tok = sem("token_index"); s_add = sem("added")

        block = ctx.enter_context(nc.Block())

        def pipeline(eng, iteration):
            def stages(i):
                return ([0 <= i - k < NT for k in range(5)]
                        + [i % 2 == 1 and 5 <= i <= NT + 3, i % 2 == 0 and 6 <= i <= NT + 4])

            for i in range(PEEL):
                iteration(i, i // 2, i, i % 4, *stages(i))
            with eng.Fori(PEEL // 4, NT // 4 - 1) as turn:
                for k in range(PEEL, PEEL + 4):
                    iteration(turn * 4 + (k - 4), turn * 2 + (k // 2 - 2), PEEL, k % 4, *stages(k))
            for i in range(NT - 2, NT + 5):
                iteration(i, i // 2, i, i % 4, *stages(i))

        @block.sync
        def _(sp):
            sp.dma_start(patch_sb[:, 0:3, :], patches[:, 0:3, :]).then_inc(s_patch, 16)
            sp.dma_start(tokw_sb[:, :, :], tokw).then_inc(s_tokw, 16)
            sp.dma_start(patch_sb[:, 3:6, :], patches[:, 3:6, :]).then_inc(s_patch, 16)
            sp.dma_start(posb_sb[:, :], posb).then_inc(s_posb, 16)
            sp.dma_start(tokb_sb[:, :], tokb).then_inc(s_posb, 16)
            sp.dma_start(ident_sb[:, :], ident).then_inc(s_const, 16)
            sp.wait_ge(s_gaps, 1)
            tx = txt.rearrange("(t two) s d -> two s t d", two=2)
            for two in range(2):
                at = two * HALF + NPATCH
                sp.dma_start(h_all[at:at + NTXT, :, :], tx[two]).then_inc(s_txt, 16)
            sp.dma_start(rope_sb[:, :, :], rope.rearrange("p (a b) -> p a b", a=2)).then_inc(s_const, 16)
            sp.dma_start(mask_sb[:, :, :], mask.rearrange("p (a b) -> p a b", a=HEADS)).then_inc(s_const, 16)
            sp.dma_start(small_sb[:, :], small).then_inc(s_const, 16)
            sp.dma_start(orderf_sb[:, :], order).then_inc(s_const, 16)
            sp.dma_start(wqkv0_sb[:, :], wqkv[0:P, :]).then_inc(s_wqkv, 16)
            sp.dma_start(wqkv1_sb[:, :], wqkv[P:D + 1, :]).then_inc(s_wqkv, 16)
            sp.dma_start(wo0_sb[:, :], wo[0:P, :]).then_inc(s_wo, 16)
            sp.dma_start(wo1_sb[:, :], wo[P:D + 1, :]).then_inc(s_wo, 16)
            sp.dma_start(gate_sb[:, 0, :], gate[0:P, :]).then_inc(s_wo, 16)
            sp.dma_start(gate_sb[0:D1, 1, :], gate[P:D, :]).then_inc(s_wo, 16)
            sp.wait_ge(s_ptok, 4)
            sp.dma_start(fused.rearrange("(g p) d -> p g d", p=P), ptok_sb[:, :, :]).then_inc(s_ptok_out, 16)
            sp.wait_ge(s_ptok_out, 16)
            fu = fused.rearrange("(t two s) d -> two s t d", two=2, s=NPATCH)
            for two in range(2):
                sp.dma_start(h_all[two * HALF:two * HALF + NPATCH, :, :], fu[two]).then_inc(s_ptok_in, 16)
            sp.wait_ge(s_zero, 1)
            sp.dma_start(out[N:N + CAP, :].rearrange("(c p) d -> p c d", p=CR),
                         zero_sb[0:CR, 0:CC, 0:D]).then_inc(s_h_out, 16)
            sp.dma_start(nw0_sb[:, :], normw[0:P, :]).then_inc(s_nw, 16)
            for lo in (0, D1):
                sp.dma_start(nw1_sb[lo:lo + D1, :], normw[P:D, :]).then_inc(s_nw, 16)

            def load_w13(e):
                sp.dma_start(rawa_sb[:, :], w13[bass.ds(e * D, P), :]).then_inc(s_raw, 16)
                for lo in (0, D1):
                    sp.dma_start(rawb_sb[lo:lo + D1, :], w13[bass.ds(e * D + P, D1), :]).then_inc(s_raw, 16)

            def load_w2(e, par):
                sp.dma_start(w2_sb[:, par, :, :],
                             w2[bass.ds(e * H, H), :].rearrange("(m p) d -> p m d", p=P)).then_inc(s_w2[par], 16)

            def load_slots(e, par):
                sp.dma_start(zs[:, par, :, :],
                             slots[bass.ds(e * CAP, CAP), :].rearrange("(c p) r -> p c r", p=CR)).then_inc(s_zs[par], 16)

            load_w13(0)
            load_w2(0, 0)
            load_w2(1, 1)
            sp.wait_ge(s_x2, NT)
            ho = out[0:N, :].rearrange("(b s) d -> b s d", s=S).rearrange("(t two) s d -> two s t d", two=2)
            for two in range(2):
                sp.dma_start(ho[two], h_all[two * HALF:two * HALF + S, :, :]).then_inc(s_h_out, 16)
            sp.wait_ge(s_disp, 32 * NT + 16)
            load_slots(0, 0)
            load_slots(1, 1)
            sp.wait_ge(s_wl, 2)
            load_w13(1)
            with sp.Fori(1, E // 2) as pair:
                for par in range(2):
                    e = pair * 2
                    sp.wait_ge(s_wl, 2 * (e + par))
                    load_w13(e + par)
                    sp.wait_ge(s_down, 2 * (e + (par - 1)))
                    load_w2(e + par, par)
                    sp.wait_ge(s_yw, CC * (e + (par - 1)))
                    sp.wait_ge(s_tok, e + (par - 1))
                    load_slots(e + par, par)

        @block.tensor
        def _(pe):
            pe.wait_ge(s_tokw, 16)
            pe.wait_ge(s_patch, 32)
            for g in range(4):
                for k in range(PK):
                    mm = pe.matmul(bank[g][:, 0:D], patch_sb[:, k, g * P:(g + 1) * P], tokw_sb[:, k, :],
                                   start=(k == 0), stop=(k == PK - 1))
                mm.then_inc(s_pe_tok, 1)
            pe.wait_ge(s_const, 16 * 5)
            pe.wait_ge(s_wqkv, 32)
            pe.wait_ge(s_wo, 64)
            pe.wait_ge(s_ones, 1)
            pe.wait_ge(s_ptok, 4)

            def iteration(i, half, i0, quad, a, b, c, d, m, r1, r2):
                par = quad % 2
                if a:
                    pe.wait_ge(s_xn, i + 1)
                    if i0 >= 1:
                        pe.wait_ge(s_rope, i)
                    pe.transpose(bank[4][:, 0:P], xn[:, 0:D0], ident_sb[:, :])
                    pe.transpose(bank[4][0:D1, P:2 * P], xn[:, D0:D], ident_sb[:, :]).then_inc(s_xt, 1)
                if b:
                    pe.wait_ge(s_qkT, 5 * i)
                    if i0 >= 2:
                        pe.wait_ge(s_pT, 2 * (i - 1))
                    q = 1 - par
                    for g in range(HG):
                        for two in range(2):
                            lo = two * HALF
                            mm = pe.matmul(bank[g // 2][lo:lo + HALF, (g % 2) * 4 * S:(g % 2 + 1) * 4 * S],
                                           qT[:, q, g, lo:lo + HALF],
                                           kbd[:, q, two, g, :, :].rearrange("p a b -> p (a b)"),
                                           start=True, stop=True)
                    mm.then_inc(s_sc, 1)
                if c:
                    pe.wait_ge(s_pT, 2 * (i - 1))
                    pe.wait_ge(s_v, 4 * (i - 1))
                    if i0 >= 3:
                        pe.wait_ge(s_res, i - 2)
                    for p in range(HEADS // 2):
                        for two in range(2):
                            lo = two * HALF
                            w = 2 * (HD + 1)
                            mm = pe.matmul(bank[6][lo:lo + HALF, p * w:(p + 1) * w],
                                           pT[:, par, p, lo:lo + HALF],
                                           vbd[:, par, two, p, :, :].rearrange("p a b -> p (a b)"),
                                           start=True, stop=True)
                    mm.then_inc(s_pv, 1)
                if a:
                    pe.wait_ge(s_xT, i + 1)
                    x0 = xT0[:, :, :, :].rearrange("p a b c -> p (a b c)")
                    x1 = xT1[:, :, :, :].rearrange("p a b c -> p (a b c)")
                    pe.matmul(bank[4][:, 0:2 * D], x0[:, HALF:3 * HALF], wqkv0_sb[:, 0:2 * D], start=True, stop=False)
                    pe.matmul(bank[4][:, 0:2 * D], x1[:, HALF:3 * HALF], wqkv1_sb[:, 0:2 * D], start=False, stop=True)
                    if i0 >= 1:
                        pe.wait_ge(s_v, 4 * i)
                    for two in range(2):
                        o = bank[5][:, two * D:(two + 1) * D]
                        pe.matmul(o, x0[:, two * P:(two + 1) * P], wqkv0_sb[:, 2 * D:3 * D], start=True, stop=False)
                        mm = pe.matmul(o, x1[:, two * P:(two + 1) * P], wqkv1_sb[:, 2 * D:3 * D], start=False, stop=True)
                    mm.then_inc(s_qkv, 1)
                if d:
                    pe.wait_ge(s_x2, i - 2)
                    if i0 >= 4:
                        pe.wait_ge(s_lg, i - 3)
                    if i0 >= 6 and not par:
                        pe.wait_ge(sR2, STEPS["R2"] * (half - 3) + 2)
                    pe.transpose(bank[7][:, 0:P], x2[:, 1 - par, 0:D0], ident_sb[:, :])
                    pe.transpose(bank[7][0:D1, P:2 * P], x2[:, 1 - par, D0:D], ident_sb[:, :]).then_inc(s_x2t, 1)
                if b:
                    pe.wait_ge(s_exp, i)
                    for p in range(HEADS // 2):
                        mm = pe.transpose(bank[p // 3][:, (p % 3) * P:(p % 3 + 1) * P],
                                          pr[:, 2 * p:2 * p + 2, :].rearrange("p a b -> p (a b)"), ident_sb[:, :])
                        if p % 3 == 2:
                            mm.then_inc(s_pt, 1)
                if c:
                    pe.wait_ge(s_att, i - 1)
                    pe.transpose(bank[6][:, 0:P], att[:, 0:D0], ident_sb[:, :])
                    pe.transpose(bank[6][0:D1, P:2 * P], att[:, D0:D], ident_sb[:, :]).then_inc(s_ot, 1)
                if a:
                    pe.wait_ge(s_qk, i + 1)
                    for r in range(2):
                        for g in range(HG):
                            mm = pe.transpose(bank[2 + r][:, g * P:(g + 1) * P],
                                              qk[:, r, 4 * g:4 * g + 4, :].rearrange("p a b -> p (a b)"), ident_sb[:, :])
                        mm.then_inc(s_qkt, 1)
                if d:
                    pe.wait_ge(s_x2T, i - 2)
                elif r1:
                    pe.wait_ge(s_lg, i - 3)
                if r1:
                    pe.wait_ge(s_hots, half - 1)
                    p0 = 2 * P
                    pe.matmul(bank[7][:, p0:p0 + E], order_sb[:, 0:P], hots[:, 0, :], start=True, stop=True)
                    pe.matmul(bank[7][:, p0 + E:p0 + 2 * E], order_sb[:, 0:P], hots[:, 1, :], start=True, stop=False)
                    pe.matmul(bank[7][:, p0 + E:p0 + 2 * E], order_sb[:, P:2 * P], hots[:, 0, :], start=False, stop=True)
                    pe.matmul(bank[7][:, p0 + 2 * E:p0 + 3 * E], order_sb[:, P:2 * P], hots[:, 0, :], start=True, stop=False)
                    pe.matmul(bank[7][:, p0 + 2 * E:p0 + 3 * E], order_sb[:, P:2 * P], hots[:, 1, :],
                              start=False, stop=True).then_inc(s_pos, 1)
                if d:
                    pe.matmul(bank[7][:, 0:E], x2T0[:, :], gate_sb[:, 0, :], start=True, stop=False)
                    pe.matmul(bank[7][:, 0:E], x2T1[:, :], gate_sb[0:D1, 1, :], start=False, stop=True).then_inc(s_gate, 1)
                if c:
                    pe.wait_ge(s_oT, i - 1)
                    pe.matmul(bank[6][:, 0:D], oT0[:, :], wo0_sb[:, :], start=True, stop=False)
                    pe.matmul(bank[6][:, 0:D], oT1[:, :], wo1_sb[:, :], start=False, stop=True).then_inc(s_proj, 1)

            pipeline(pe, iteration)

            def turn(e, par):
                for n, (zn, wide) in enumerate(((zn0, "c d -> c d"), (zn1, "c a d -> c (a d)"))):
                    pe.wait_ge(s_zn, 2 * e + (n + 1))
                    for c in range(CC):
                        mm = pe.transpose(bank[4 + n][:, c * CR:(c + 1) * CR], zn[:, c].rearrange(wide),
                                          ident_sb[0:CR, 0:CR])
                    mm.then_inc(s_zt, 1)

            def expert(e, e0, par, more):
                pe.wait_ge(s_wl, 2 * (e + 1))
                pe.wait_ge(s_z, 2 * (e + 1))
                for m in range(MH):
                    q = 2 * (m % 2)
                    if e0 >= 1 or m >= 2:
                        pe.wait_ge(s_hT, MH * e + m - 1)
                    for r in range(2):
                        cols = slice(r * H + m * P, r * H + (m + 1) * P)
                        o = bank[q + r][:, 0:CAP]
                        pe.matmul(o, wah[:, par, cols], z0h[:, par, :], start=True, stop=False)
                        pe.matmul(o, wah[:, par, cols], z0l[:, par, :], start=False, stop=False)
                        pe.matmul(o, wal[:, par, cols], z0h[:, par, :], start=False, stop=False)
                        pe.matmul(o, wbh[:, par, cols], z1[:, par, :], start=False, stop=False)
                        mm = pe.matmul(o, wbl[:, par, cols], z1[0:D1, par, :], start=False, stop=True)
                    mm.then_inc(s_up, 1)
                if more:
                    turn(e + 1, 1 - par)
                pe.wait_ge(s_w2[par], 8 * (e - par) + 16)
                pe.wait_ge(s_hT, MH * (e + 1))
                for c in range(CC):
                    if c % 2 == 0 and e0 >= 1:
                        pe.wait_ge(s_yx, 2 * e + (c // 2 - 1))
                    for m in range(MH):
                        mm = pe.matmul(bank[6 + c // 2][0:CR, (c % 2) * D:(c % 2 + 1) * D],
                                       hT[:, m, c * CR:(c + 1) * CR], w2_sb[:, par, m, :],
                                       start=(m == 0), stop=(m == MH - 1))
                    if c % 2 == 1:
                        mm.then_inc(s_down, 1)

            turn(0, 0)
            expert(0, 0, 0, True)
            expert(1, 1, 1, True)
            with pe.Fori(1, E // 2 - 1) as pair:
                expert(pair * 2, 2, 0, True)
                expert(pair * 2 + 1, 3, 1, True)
            expert(E - 2, E - 2, 0, True)
            expert(E - 1, E - 1, 1, False)

        @block.scalar
        def _(act):
            act.wait_ge(s_ones, 1)

            def iteration(i, half, i0, quad, a, b, c, d, m, r1, r2):
                par = quad % 2
                if a:
                    act.wait_ge(s_xt, i + 1)
                    if i0 >= 1:
                        act.wait_ge(s_qkv, i)
                    for n, xT, at in ((P, xT0, 0), (D1, xT1, P)):
                        turned = bank[4][0:n, at:at + P].rearrange("p (a c) -> p a c", a=2)
                        ins = act.copy(xT[0:n, :, :, :], turned.unsqueeze(2).to_broadcast([n, 2, 2, HALF]))
                    ins.then_inc(s_xT, 1)
                if b:
                    act.wait_ge(s_sh, i)
                    if i0 >= 2:
                        act.wait_ge(s_pt, 2 * (i - 1))
                    act.activation(pr[:, :, 0:S], sm[:, :].rearrange("p (h k) -> p h k", k=S), ACT.Exp).then_inc(s_exp, 1)
                if a:
                    act.wait_ge(s_qkv, i + 1)
                    if i0 >= 2:
                        act.wait_ge(s_pv, i - 1)
                    for two in range(2):
                        for odd in range(2):
                            lo = odd * HALF
                            act.copy(vbd[lo:lo + HALF, par, two, :, odd, 0:HD],
                                     bank[5][lo:lo + HALF, two * D:(two + 1) * D].rearrange(
                                         "p (a b d) -> p a b d", b=2, d=HD)[:, :, odd, :]).then_inc(s_v, 1)
                if d:
                    act.wait_ge(s_x2, i - 2)
                    if i0 >= 5:
                        act.wait_ge(s_ms, i - 4)
                    act.activation(squares[:, :], x2[:, 1 - par, :], ACT.Square, scale=D ** -0.5,
                                   accum_out=ssq[:, 1 - par:2 - par]).then_inc(s_ssq, 1)
                    if i0 >= 6:
                        act.wait_ge(s_disp, 32 * (i - 6) + 16)
                    act.copy(rows[:, (quad + 1) % 4, 0:D],
                             x2[:, 1 - par, :]).then_inc(s_rowx, 1)
                if b:
                    for r in range(2):
                        act.wait_ge(s_pt, 2 * (i - 1) + r + 1)
                        if r == 0 and i0 >= 3:
                            act.wait_ge(s_pv, i - 2)
                        act.copy(pT[:, 1 - par, 3 * r:3 * r + 3, :].rearrange("p a b -> p (a b)"),
                                 bank[r][:, 0:3 * P]).then_inc(s_pT, 1)
                if d:
                    act.wait_ge(s_x2t, i - 2)
                    if i0 >= 4:
                        act.wait_ge(s_gate, i - 3)
                    act.copy(x2T0[:, :], bank[7][:, 0:P])
                    act.copy(x2T1[:, :], bank[7][0:D1, P:2 * P]).then_inc(s_x2T, 1)
                if c:
                    act.wait_ge(s_ot, i - 1)
                    if i0 >= 3:
                        act.wait_ge(s_proj, i - 2)
                    act.copy(oT0[:, :], bank[6][:, 0:P])
                    act.copy(oT1[0:D1, :], bank[6][0:D1, P:2 * P]).then_inc(s_oT, 1)
                if r1:
                    act.wait_ge(s_diff, half - 1)
                    if i0 >= 6:
                        act.wait_ge(sR2, STEPS["R2"] * (half - 2))
                    act.activation(ratio[:, :], gapd[:, :], ACT.Exp).then_inc(s_ratio, 1)
                if a:
                    act.wait_ge(s_qkt, 2 * i + 1)
                    if i0 >= 2:
                        act.wait_ge(s_sc, i - 1)
                    act.copy(qT[:, par, :, :].rearrange("p a b -> p (a b)"), bank[2][:, 0:3 * P]).then_inc(s_qkT, 1)
                    act.wait_ge(s_qkt, 2 * i + 2)
                    for j in range(4):
                        rows_k = bank[3][32 * j:32 * j + 32, 0:3 * P].rearrange("p (g two k) -> p two g k", g=HG, two=2)
                        act.copy(kbd[32 * j:32 * j + 32, par, :, :, j, :], rows_k[:, :, :, 0:S]).then_inc(s_qkT, 1)

            pipeline(act, iteration)

            def prepare(e, e0, par):
                act.wait_ge(s_zt, 2 * e + 1)
                if e0 >= 2:
                    act.wait_ge(s_up, MH * (e - 1))
                act.mul(z0h[:, par, :], bank[4][:, 0:CAP], nw0_sb[:, bass.ds(e, 1)]).then_inc(s_zh, 1)
                act.wait_ge(s_zt, 2 * e + 2)
                act.mul(z1[:, par, :], bank[5][:, 0:CAP], nw1_sb[:, bass.ds(e, 1)]).then_inc(s_zh, 1)

            def split_high(e, e0, par, n):
                if n == 0:
                    act.wait_ge(s_raw, 48 * (e + 1))
                act.copy((wah, wbh)[n][:, par, :], (rawa_sb, rawb_sb)[n][:, :]).then_inc(s_wh, 1)

            def expert(e, e0, par, more):
                for m in range(MH):
                    act.wait_ge(s_up, MH * e + m + 1)
                    if e0 >= 1 or m >= 2:
                        act.wait_ge(s_hT, MH * e + m - 1)
                    act.activation(sg[:, m % 2, :], bank[2 * (m % 2)][:, 0:CAP], ACT.Silu).then_inc(s_silu, 1)
                    if more and m < 2:
                        split_high(e + 1, e0 + 1, 1 - par, m)
                if more:
                    prepare(e + 1, e0 + 1, 1 - par)
                for c in range(CC):
                    act.wait_ge(s_yx, 2 * e + c // 2 + 1)
                    if e0 >= 1 and c == 0:
                        act.wait_ge(s_add, 64 * e)
                    act.mul(yw[:, c, :], yx[:, c, :], zs[:, par, c, bass.ds(e + W_COL, 1)]).then_inc(s_yw, 1)

            act.wait_ge(s_nw, 48)
            for n in range(2):
                split_high(0, 0, 0, n)
            prepare(0, 0, 0)
            expert(0, 0, 0, True)
            expert(1, 1, 1, True)
            with act.Fori(1, E // 2 - 1) as pair:
                expert(pair * 2, 2, 0, True)
                expert(pair * 2 + 1, 3, 1, True)
            expert(E - 2, E - 2, 0, True)
            expert(E - 1, E - 1, 1, False)

        @block.vector
        def _(dve):
            dve.memset(zero_sb[:, :, :], 0.0).then_inc(s_pre, 1)
            dve.wait_ge(s_pre, 1)
            dve.memset(xT1[D1:D1 + 1, :, :, :], 1.0)
            dve.memset(oT1[D1:D1 + 1, :], 1.0)
            dve.memset(qk[:, :, :, :], 0.0)
            dve.memset(kbd[:, :, :, :, :, :], 0.0)
            dve.memset(pr[:, :, :], 0.0)
            dve.memset(count[:, :], 0.0)
            dve.memset(vbd[:, :, :, :, :, :], 0.0).then_inc(s_pre, 1)
            dve.wait_ge(s_pre, 2)
            dve.memset(vbd[0:HALF, :, :, :, 0, HD:HD + 1], 1.0)
            dve.memset(vbd[HALF:P, :, :, :, 1, HD:HD + 1], 1.0).then_inc(s_ones, 1)
            dve.wait_ge(s_posb, 32)
            dve.tensor_tensor(posb_sb[:, :], posb_sb[:, :], tokb_sb[:, :], ALU.add).then_inc(s_posum, 1)
            dve.wait_ge(s_posum, 1)
            for g in range(4):
                dve.wait_ge(s_pe_tok, g + 1)
                dve.tensor_tensor(ptok_sb[:, g, :], bank[g][:, 0:D], posb_sb[:, :], ALU.add).then_inc(s_ptok, 1)
            dve.wait_ge(s_const, 16 * 5)
            dve.tensor_copy(zero_sb[:, :, ID_COL], small_sb[:, SPARE0:SPARE0 + SPP]).then_inc(s_zero, 1)
            dve.tensor_copy(order_sb[:, :], orderf_sb[:, :]).then_inc(s_order, 1)
            dve.wait_ge(s_gaps, 1)
            dve.wait_ge(s_txt, 32)
            dve.wait_ge(s_ptok_in, 32)
            for t in range(NT):
                ins = dve.bn_stats(stats[:, t, :], h_all[:, t, :])
            ins.then_inc(s_pre, 1)
            dve.wait_ge(s_pre, 3)
            for t in range(NT):
                ins = dve.bn_aggr(mv[:, t, :], stats[:, t, :])
            ins.then_inc(s_pre, 1)
            dve.wait_ge(s_pre, 4)
            dve.tensor_scalar(ve1[:, :], mv[:, :, 1], LN_EPS, None, ALU.add).then_inc(s_stat, 1)
            dve.wait_ge(s_rstd1, 1)

            def norm1(t, t0):
                if t0 >= 1:
                    dve.wait_ge(s_xt, t)
                dve.tensor_scalar(xn[:, :], h_all[:, bass.ds(t, 1), :].rearrange("p a d -> p (a d)"),
                                  mv[:, bass.ds(t, 1), 0], rstd1[:, bass.ds(t, 1)],
                                  ALU.subtract, ALU.mult).then_inc(s_xn, 1)

            def steps(sem_, name, t):
                k = [0]

                def link(ins, wait=True):
                    k[0] += 1
                    ins.then_inc(sem_, 1)
                    if wait:
                        dve.wait_ge(sem_, STEPS[name] * t + k[0])

                def done():
                    assert k[0] == STEPS[name], (name, k[0])
                return link, done

            norm1(0, 0)

            def iteration(i, half, i0, quad, a, b, c, d, m, r1, r2):
                par = quad % 2
                if m:
                    dve.wait_ge(s_gate, i - 3)
                    dve.tensor_copy(lg[:, :], bank[7][:, 0:E]).then_inc(s_lg, 1)
                if r2:
                    link_r2, done_r2 = steps(sR2, "R2", half - 3)
                    dve.wait_ge(s_pos, half - 2)
                    p0 = 2 * P
                    link_r2(dve.tensor_tensor(pos[:, :, :], bank[7][:, p0:p0 + 2 * E].rearrange("p (a e) -> p a e", a=2),
                                              count[:, :].unsqueeze(1).to_broadcast([P, 2, E]), ALU.add))
                    link_r2(dve.tensor_tensor(count[:, :], bank[7][:, p0 + 2 * E:p0 + 3 * E], count[:, :], ALU.add),
                            wait=False)
                if b:
                    link, done = steps(sB, "B", i - 1)
                    dve.wait_ge(s_sc, i)
                    if i0 >= 2:
                        dve.wait_ge(s_exp, i - 1)
                    dve.tensor_tensor(sm[:, 0:8 * S], bank[0][:, 0:8 * S],
                                      mask_sb[:, 0:8, :].rearrange("p a b -> p (a b)"), ALU.add)
                    dve.tensor_tensor(sm[:, 8 * S:12 * S], bank[1][:, 0:4 * S],
                                      mask_sb[:, 8:12, :].rearrange("p a b -> p (a b)"), ALU.add).then_inc(s_scread, 1)
                    dve.wait_ge(s_scread, i)
                    sm3 = sm[:, :].rearrange("p (h k) -> p h k", k=S)
                    link(dve.tensor_reduce(mx[:, :], sm3, AX.X, ALU.max))
                    dve.tensor_tensor(sm3, sm3, mx[:, :].unsqueeze(2).to_broadcast([P, HEADS, S]),
                                      ALU.subtract).then_inc(s_sh, 1)
                    done()
                if d:
                    dve.wait_ge(s_rstd2, i - 2)
                    if i0 >= 5:
                        dve.wait_ge(s_rowx, i - 4)
                        dve.wait_ge(s_x2t, i - 4)
                    dve.tensor_scalar(x2[:, 1 - par, :], h_all[:, bass.ds(i - 3, 1), :].rearrange("p a d -> p (a d)"),
                                      mv2[:, 0:1], rstd2[:, :], ALU.subtract, ALU.mult).then_inc(s_x2, 1)
                if a:
                    dve.wait_ge(s_qkv, i + 1)
                    if i0 >= 1:
                        dve.wait_ge(s_qk, i)
                    q2 = bank[4][:, 0:2 * D]
                    dve.tensor_tensor(rc[:, :], q2, rope_sb[:, 0, :], ALU.mult)
                    pairs = q2.rearrange("p (n two) -> p n two", two=2)
                    rs2 = rs[:, :].rearrange("p (n two) -> p n two", two=2)
                    sn2 = rope_sb[:, 1, :].rearrange("p (n two) -> p n two", two=2)
                    dve.tensor_tensor(rs2[:, :, 0], pairs[:, :, 1], sn2[:, :, 0], ALU.mult)
                    dve.tensor_tensor(rs2[:, :, 1], pairs[:, :, 0], sn2[:, :, 1], ALU.mult).then_inc(s_rope, 1)
                if c:
                    link, done = steps(sC, "C", i - 2)
                    dve.wait_ge(s_pv, i - 1)
                    o4 = bank[6][:, 0:HEADS * (HD + 1)].rearrange("p (h d) -> p h d", h=HEADS)
                    link(dve.reciprocal(rden[:, :], o4[:, :, HD]))
                    if i0 >= 3:
                        dve.wait_ge(s_ot, i - 2)
                    dve.tensor_tensor(att[:, :].rearrange("p (h d) -> p h d", h=HEADS), o4[:, :, 0:HD],
                                      rden[:, :].unsqueeze(2).to_broadcast([P, HEADS, HD]),
                                      ALU.mult).then_inc(s_att, 1)
                if a and i0 + 1 < NT:
                    norm1(i + 1, i0 + 1)
                if m:
                    q = par
                    dve.wait_ge(s_ones, 1)
                    dve.wait_ge(s_lg, i - 3)
                    dve.max(top[:, q, :], lg[:, :]).then_inc(s_top, 1)
                    dve.wait_ge(s_ones, 1)
                    dve.wait_ge(s_top, i - 3)
                    dve.max_index(choice[:, q, :], top[:, q, :], lg[:, :]).then_inc(s_choice, 1)
                    dve.wait_ge(s_choice, i - 3)
                    dve.tensor_copy(chosen[:, 2 * q:2 * q + 2], choice[:, q, 0:2]).then_inc(s_chosen, 1)
                    if r1:
                        dve.wait_ge(s_chosen, i - 3)
                if r1:
                    link, done = steps(sR1, "R1", half - 2)
                    dve.tensor_tensor(gapd[:, :], top[:, :, 1], top[:, :, 0], ALU.subtract).then_inc(s_diff, 1)
                    ex = small_sb[:, EXP0:EXP0 + E].unsqueeze(1).to_broadcast([P, 4, E])
                    link(dve.tensor_tensor(hot[:, :, :, :].rearrange("p a b e -> p (a b) e"), ex,
                                           chosen[:, :].unsqueeze(2).to_broadcast([P, 4, E]), ALU.is_equal))
                    dve.tensor_tensor(hots[:, :, :], hot[:, :, 0, :], hot[:, :, 1, :], ALU.add).then_inc(s_hots, 1)
                    link(dve.tensor_scalar(base[:, :], chosen[:, :], float(CAP), small_sb[:, GAP0:GAP0 + 1],
                                           ALU.mult, ALU.add), wait=False)
                    link(dve.tensor_copy(over[:, :], chosen[:, :]), wait=False)
                    done()
                if r2:
                    link, done = link_r2, done_r2
                    dve.wait_ge(sR2, STEPS["R2"] * (half - 3) + 2)
                    dve.tensor_tensor(posk[:, :, :, :], hot[:, :, :, :],
                                      pos[:, :, :].unsqueeze(2).to_broadcast([P, 2, 2, E]), ALU.mult)
                    dve.wait_ge(s_ratio, half - 2)
                    link(dve.tensor_scalar(total[:, :], ratio[:, :], 1.0, None, ALU.add))
                    link(dve.tensor_reduce(pk[:, :], posk[:, :, :, :].rearrange("p a b e -> p (a b) e"), AX.X, ALU.add),
                         wait=False)
                    link(dve.reciprocal(wts[:, :, 0], total[:, :]))
                    link(dve.tensor_tensor(base[:, :], base[:, :], pk[:, :], ALU.add), wait=False)
                    dve.tensor_tensor(wts[:, :, 1], wts[:, :, 0], ratio[:, :], ALU.mult)
                    link(dve.tensor_scalar(over[:, :], pk[:, :], float(CAP), FAR, ALU.is_ge, ALU.mult))
                    if i0 >= 6:
                        dve.wait_ge(s_disp, 64 * (half - 3) + 16)
                    dve.tensor_tensor(slot[:, :],
                                      over[:, :], base[:, :], ALU.add)
                    link(dve.tensor_tensor(wk[:, :, :, :], hot[:, :, :, :],
                                           wts[:, :, :].unsqueeze(3).to_broadcast([P, 2, 2, E]), ALU.mult))
                    dve.tensor_tensor(rows[:, (quad + 2) % 4:(quad + 2) % 4 + 2, W_COL:W_COL + E], wk[:, :, 0, :], wk[:, :, 1, :],
                                      ALU.add).then_inc(s_slot, 1)
                    done()
                if c:
                    dve.wait_ge(s_proj, i - 1)
                    ht = h_all[:, bass.ds(i - 2, 1), :].rearrange("p a d -> p (a d)")
                    dve.tensor_tensor(ht, bank[6][:, 0:D], ht, ALU.add).then_inc(s_res, 1)
                    dve.wait_ge(s_ones, 1)
                    dve.wait_ge(s_res, i - 1)
                    dve.bn_stats(st2[:, :], ht).then_inc(s_st2, 1)
                    dve.wait_ge(s_ones, 1)
                    dve.wait_ge(s_st2, i - 1)
                    dve.bn_aggr(mv2[:, :], st2[:, :]).then_inc(s_mv2, 1)
                    dve.wait_ge(s_mv2, i - 1)
                    if i0 >= 3:
                        dve.wait_ge(s_rstd2, i - 2)
                    dve.tensor_scalar(ve2[:, :], mv2[:, 1:2], LN_EPS, None, ALU.add).then_inc(s_var2, 1)
                    done()

            pipeline(dve, iteration)

            def scale(e, e0, par):
                dve.wait_ge(s_zs[par], 8 * (e - par) + 16)
                if e0 >= 1:
                    dve.wait_ge(s_zt, 2 * e)
                dve.tensor_copy(tok[:, bass.ds(e, 1), :], zs[:, par:par + 1, :, ID_COL]).then_inc(s_tok, 1)
                rms = zs[:, par, :, RMS_COL:RMS_COL + 1]
                dve.tensor_tensor(zn0[:, :, :], zs[:, par, :, 0:D0], rms.to_broadcast([CR, CC, D0]),
                                  ALU.mult).then_inc(s_zn, 1)
                dve.tensor_tensor(zn1[:, :, :, :], zs[:, par, :, D0:D].unsqueeze(2).to_broadcast([CR, CC, 2, D1]),
                                  rms.unsqueeze(3).to_broadcast([CR, CC, 2, D1]), ALU.mult).then_inc(s_zn, 1)

            def split_rest(par, e, n):
                dve.wait_ge(s_wh, 2 * e + (n + 1))
                if n == 0:
                    dve.tensor_tensor(wal[:, par, :], rawa_sb[:, :], wah[:, par, :].bitcast(F32), ALU.subtract).then_inc(s_wl, 1)
                else:
                    dve.tensor_tensor(wbl[:, par, :], rawb_sb[0:D1, :], wbh[0:D1, par, :].bitcast(F32),
                                      ALU.subtract).then_inc(s_wl, 1)

            def z_rest(e, par):
                dve.wait_ge(s_zh, 2 * e + 1)
                dve.scalar_tensor_tensor(z0l[:, par, :], bank[4][:, 0:CAP], nw0_sb[:, bass.ds(e, 1)],
                                         z0h[:, par, :].bitcast(F32), ALU.mult, ALU.subtract).then_inc(s_z, 1)
                dve.wait_ge(s_zh, 2 * e + 2)
                low = z1[D1:P, par, :]
                dve.scalar_tensor_tensor(low, bank[5][D1:P, 0:CAP], nw1_sb[D1:P, bass.ds(e, 1)],
                                         low.bitcast(F32), ALU.mult, ALU.subtract).then_inc(s_z, 1)

            def expert(e, e0, par, more):
                if more:
                    scale(e + 1, e0 + 1, 1 - par)
                for m in range(MH):
                    dve.wait_ge(s_silu, MH * e + m + 1)
                    if e0 >= 1 and m == 0:
                        dve.wait_ge(s_down, 2 * e)
                    dve.tensor_tensor(hT[:, m, :], sg[:, m % 2, :], bank[2 * (m % 2) + 1][:, 0:CAP],
                                      ALU.mult).then_inc(s_hT, 1)
                    if more and 1 <= m <= 2:
                        split_rest(1 - par, e + 1, m - 1)
                if more:
                    z_rest(e + 1, 1 - par)
                for r in range(2):
                    dve.wait_ge(s_down, 2 * e + r + 1)
                    if e0 >= 1 and r == 0:
                        dve.wait_ge(s_yw, CC * e)
                    dve.tensor_tensor(yx[:, 2 * r:2 * r + 2, :],
                                      bank[6 + r][0:CR, 0:2 * D].rearrange("p (a d) -> p a d", a=2),
                                      zs[:, par, 2 * r:2 * r + 2, 0:D], ALU.add).then_inc(s_yx, 1)

            for n in range(2):
                split_rest(0, 0, n)
            scale(0, 0, 0)
            z_rest(0, 0)
            expert(0, 0, 0, True)
            expert(1, 1, 1, True)
            with dve.Fori(1, E // 2 - 1) as pair:
                expert(pair * 2, 2, 0, True)
                expert(pair * 2 + 1, 3, 1, True)
            expert(E - 2, E - 2, 0, True)
            expert(E - 1, E - 1, 1, False)

        @block.gpsimd
        def _(pool):
            pool.memset(h_all[32:64, :, :], 0.0)
            pool.memset(h_all[96:P, :, :], 0.0).then_inc(s_gaps, 1)
            pool.wait_ge(s_zero, 1)
            pool.dma_start(slots.rearrange("(p r) c -> p r c", p=P), zero_sb[:, :, :]).then_inc(s_disp, 16)
            pool.wait_ge(s_const, 16 * 5)
            pool.wait_ge(s_stat, 1)
            pool.tensor_tensor(rstd1[:, :], ve1[:, :], small_sb[:, POW0:POW0 + NT], ALU.pow).then_inc(s_rstd1, 1)

            def iteration(i, half, i0, quad, a, b, c, d, m, r1, r2):
                par = quad % 2
                if d:
                    q = 1 - par
                    pool.wait_ge(s_ssq, i - 2)
                    pool.tensor_tensor(ms[:, q:q + 1], ssq[:, q:q + 1], small_sb[:, EPS0:EPS0 + 1],
                                       ALU.add).then_inc(s_ms, 1)
                    pool.wait_ge(s_ms, i - 2)
                    if i0 >= 6:
                        pool.wait_ge(s_disp, 32 * (i - 6) + 16)
                        pool.wait_ge(s_ms, i - 2)
                    r = (quad + 1) % 4
                    pool.tensor_copy(rows[:, r, ID_COL:ID_COL + 1], small_sb[:, bass.ds(i + (IDS0 - 3), 1)])
                    pool.tensor_tensor(rows[:, r, RMS_COL:RMS_COL + 1], ms[:, q:q + 1],
                                       small_sb[:, POW0:POW0 + 1], ALU.pow).then_inc(s_rms, 1)
                if a:
                    pool.wait_ge(s_rope, i + 1)
                    if i0 >= 1:
                        pool.wait_ge(s_qkt, 2 * i)
                    if i0 == PEEL:
                        pool.wait_ge(s_hots, half - 2)
                        pool.wait_ge(s_rowx, i - 5)
                    pool.tensor_tensor(qk[:, :, :, 0:HD].rearrange("p a h d -> p (a h) d"),
                                       rc[:, :].rearrange("p (h d) -> p h d", d=HD),
                                       rs[:, :].rearrange("p (h d) -> p h d", d=HD), ALU.add).then_inc(s_qk, 1)
                if i0 == PEEL:
                    pool.wait_ge(s_disp, 16)
                for t, q in ([(i - 6, par)] if i0 >= 6 else []) + ([(i - 5, 1)] if i0 == NT + 4 else []):
                    pool.wait_ge(s_ones, 1)
                    pool.wait_ge(s_slot, half - 2)
                    pool.wait_ge(s_rms, t + 1)
                    pool.wait_ge(s_rowx, t + 1)
                    for k in range(2):
                        pool.indirect_dma_start(
                            out=slots, out_offset=bass.IndirectOffsetOnAxis(
                                ap=slot[:, 2 * q + k:2 * q + k + 1], axis=0),
                            in_=rows[:, (quad + 2 + (q - par)) % 4, :], in_offset=None,
                            bounds_check=E * CAP - 1, oob_is_err=False).then_inc(s_disp, 16)
                if c:
                    pool.wait_ge(s_var2, i - 1)
                    if i0 >= 3:
                        pool.wait_ge(s_x2, i - 2)
                    pool.tensor_tensor(rstd2[:, :], ve2[:, :], small_sb[:, POW0:POW0 + 1],
                                       ALU.pow).then_inc(s_rstd2, 1)

            pipeline(pool, iteration)

            pool.wait_ge(s_h_out, 48)
            for e in range(E):
                pool.wait_ge(s_tok, e + 1)
                if e >= 1:
                    pool.wait_ge(s_add, 64 * e)
                for c in range(CC):
                    pool.wait_ge(s_yw, CC * e + c + 1)
                    pool.indirect_dma_start(
                        out=out, out_offset=bass.IndirectOffsetOnAxis(ap=tok[:, e, c:c + 1], axis=0),
                        in_=yw[:, c, :], in_offset=None,
                        bounds_check=N + CAP - 1, oob_is_err=True, compute_op=ALU.add).then_inc(s_add, 16)
            pool.wait_ge(s_add, 64 * E)


_INS = ["patches", "txt", "posb", "tokb", "tokw", "wqkv", "wo", "gate", "w13", "w2", "normw",
        "rope", "mask", "small", "order", "ident"]


def kernel(x, txt, L0_tok_W, L0_tok_b, L0_tok_pos_emb, L0_attn_Wq, L0_attn_bq, L0_attn_Wk, L0_attn_bk,
           L0_attn_Wv, L0_attn_bv, L0_attn_Wo, L0_attn_bo, L0_ffn_gate_w, L0_ffn_w13, L0_ffn_w2,
           L0_ffn_norm_w):
    import concourse.bacc as bacc
    from concourse.bass_utils import run_bass_kernel_spmd

    g = IMG // PATCH
    a = {k: np.asarray(v) for k, v in locals().copy().items() if isinstance(v, np.ndarray) or hasattr(v, "dtype")}
    flat = a["x"].reshape(B, g, PATCH, g, PATCH, CH).transpose(2, 4, 5, 0, 1, 3).reshape(PK, P, B * NPATCH)
    arrays = {
        "patches": flat.transpose(1, 0, 2),
        "txt": a["txt"],
        "posb": np.tile(a["L0_tok_pos_emb"], (P // NPATCH, 1)),
        "tokb": np.tile(a["L0_tok_b"][None, :], (P, 1)),
        "tokw": a["L0_tok_W"].reshape(PK, P, D).transpose(1, 0, 2),
        "wqkv": np.concatenate([
            np.concatenate([a["L0_attn_Wq"], a["L0_attn_Wk"], a["L0_attn_Wv"]], axis=1),
            np.concatenate([a["L0_attn_bq"], a["L0_attn_bk"], a["L0_attn_bv"]])[None, :]], axis=0),
        "wo": np.concatenate([a["L0_attn_Wo"], a["L0_attn_bo"][None, :]], axis=0),
        "gate": a["L0_ffn_gate_w"].T,
        "w13": a["L0_ffn_w13"].transpose(0, 2, 1).reshape(E * D, 2 * H),
        "w2": a["L0_ffn_w2"].transpose(0, 2, 1).reshape(E * H, D),
        "normw": a["L0_ffn_norm_w"].T,
        **shape_constants(),
    }
    nc = bacc.Bacc("TRN2", target_bir_lowering=False, num_devices=1)
    feeds, args = {}, []
    for name in _INS:
        arr = np.ascontiguousarray(arrays[name])
        feeds[f"in_{name}"] = arr
        args.append(nc.dram_tensor(f"in_{name}", arr.shape, mybir.dt.from_np(arr.dtype), kind="ExternalInput").ap())
    args.append(nc.dram_tensor("out_rows", (N + CAP, D), F32, kind="ExternalOutput").ap())
    build(nc, *args)
    got = run_bass_kernel_spmd(nc, [feeds], core_ids=[0]).results[0]["out_rows"]
    return got[:N].reshape(B, S, D)
```

```python
from contextlib import ExitStack

import numpy as np

import concourse.bass as bass
from concourse import mybir

F32 = mybir.dt.float32
F32R = mybir.dt.float32r
BF16 = mybir.dt.bfloat16
U32 = mybir.dt.uint32
ALU = mybir.AluOpType
ACT = mybir.ActivationFunctionType
AX = mybir.AxisListType

P = 128
B, IMG, PATCH, CH = 32, 64, 16, 3
NPATCH = (IMG // PATCH) ** 2
PDIM = PATCH * PATCH * CH
PK = PDIM // P
NTXT = 32
S = NPATCH + NTXT
D = 192
D0, D1 = P, D - P
HEADS, HD = 12, 16
HG = HEADS // 4
NT = B // 2
HALF = 64
N = B * S
E, H = 8, 512
MH = H // P
CAP = -(-5 * 2 * N // (4 * E))
CC, CR = 4, CAP // 4
ROW = D + E + 2
W_COL, ID_COL, RMS_COL = D, D + E, D + E + 1
SPP = E * CAP // P
FAR = 1.0e5
LN_EPS, RMS_EPS = 1e-5, 1e-6
assert CAP == 480 and N == 1536


def shape_constants():
    c = {}
    half = D // 2
    inv = (1.0 / np.float32(10000.0) ** (np.arange(half, dtype=np.float32) * np.float32(2.0) / np.float32(D))).astype(np.float32)
    ang = (np.arange(S, dtype=np.float32)[:, None] * inv[None, :]).astype(np.float32)
    cos, sin = np.cos(ang), np.sin(ang)
    cos2 = np.repeat(cos, 2, axis=1)
    sin2 = np.stack([-sin, sin], axis=-1).reshape(S, D)
    rope = np.zeros((P, 2, 2, D), np.float32)
    mask = np.zeros((P, S), np.float32)
    causal = np.where(np.tril(np.ones((S, S), bool)), 0.0, -1.0e30).astype(np.float32)
    for lo in (0, HALF):
        for j, scale in ((0, HD ** -0.5), (1, 1.0)):
            rope[lo:lo + S, 0, j] = cos2 * scale
            rope[lo:lo + S, 1, j] = sin2 * scale
        mask[lo:lo + S] = causal
    c["rope"] = rope.reshape(P, -1)
    c["mask"] = np.tile(mask, (1, HEADS))
    live = np.zeros(P, bool)
    live[:S] = live[HALF:HALF + S] = True
    experts = np.tile(np.arange(E, dtype=np.float32), (P, 1))
    gap = np.where(live, 0.0, FAR).astype(np.float32)[:, None]
    ids = np.full((P, NT), FAR, np.float32)
    for t in range(NT):
        ids[0:S, t] = (2 * t) * S + np.arange(S)
        ids[HALF:HALF + S, t] = (2 * t + 1) * S + np.arange(S)
    power = np.full((P, NT), -0.5, np.float32)
    power = np.concatenate([power, np.full((P, 2), RMS_EPS / 4, np.float32)], axis=1)
    spare = (N + np.arange(E * CAP) % CAP).reshape(P, SPP).astype(np.float32)
    c["small"] = np.concatenate([experts, gap, power, ids, spare], axis=1)
    before = (np.arange(P)[:, None] < np.arange(P)[None, :]) & live[:, None]
    every = np.repeat(live[:, None], P, axis=1)
    c["order"] = np.concatenate([before, every], axis=1).astype(np.float32)
    c["ident"] = np.eye(P, dtype=np.float32)
    return c


EXP0, GAP0, POW0 = 0, E, E + 1
EPS0 = POW0 + NT
IDS0 = EPS0 + 2
SPARE0 = IDS0 + NT
SMALL = SPARE0 + SPP

PEEL = 6
STAT_TILES = [(0, 1), (1, 4), (4, 8), (8, 12), (12, 16)]

STEPS = {"C": 1, "R1": 2, "R2": 8}


def build(nc, patches, txt, posb, tokb, tokw, wqkv, wo, gate, w13, w2, normw,
          rope, mask, small, order, ident, out):
    slots = nc.dram_tensor("slots", (E * CAP, ROW), F32, kind="Internal").ap()
    fused = nc.dram_tensor("patch_tokens", (3 * P, D), F32, kind="Internal").ap()
    with ExitStack() as ctx:
        def sb(name, shape, dt=F32):
            return ctx.enter_context(nc.sbuf_tensor(name, shape, dt))

        def sem(name):
            return ctx.enter_context(nc.semaphore(name))

        idle_sb = sb("idle_sb", [P, 512], BF16)
        ident_sb = sb("ident_sb", [P, P])
        rope_sb = sb("rope_sb", [P, 2, 2 * D])
        mask_sb = sb("mask_sb", [P, HEADS, S])
        small_sb = sb("small_sb", [P, SMALL])
        orderf_sb = sb("orderf_sb", [P, 2 * P])
        order_sb = sb("order_sb", [P, 2 * P], BF16)
        tokw_sb = sb("tokw_sb", [P, PK, D])
        patch_sb = sb("patch_sb", [P, PK, B * NPATCH])
        posb_sb = sb("posb_sb", [P, D])
        tokb_sb = sb("tokb_sb", [P, D])
        ptok_sb = sb("ptok_sb", [P, 4, D])
        wqkv0_sb = sb("wqkv0_sb", [P, 3 * D])
        wqkv1_sb = sb("wqkv1_sb", [D1 + 1, 3 * D])
        wo0_sb = sb("wo0_sb", [P, D])
        wo1_sb = sb("wo1_sb", [D1 + 1, D])
        gate_sb = sb("gate_sb", [P, 2, E])
        zero_sb = sb("zero_sb", [P, SPP, ROW])
        h_all = sb("h_all", [P, NT, D])
        stats = sb("stats", [P, NT, 6])
        mv = sb("mv", [P, NT, 2])
        ve1 = sb("ve1", [P, NT])
        rstd1 = sb("rstd1", [P, NT])
        xn = sb("xn", [P, D])
        xT0 = sb("xT0", [P, P])
        xT1 = sb("xT1", [D1 + 1, P])
        rc = sb("rc", [P, 2 * D])
        rs = sb("rs", [P, 2 * D])
        qk = sb("qk", [P, 2, HEADS, 32])
        qT = sb("qT", [P, 2, HG, P])
        kbd = sb("kbd", [P, 2, 2, HG, 4, S])
        vbd = sb("vbd", [P, 2, 2, HEADS // 2, 2, HD + 1])
        sm = sb("sm", [P, HEADS * S])
        mx = sb("mx", [P, HEADS])
        pr = sb("pr", [P, HEADS, 64])
        pT = sb("pT", [P, 2, HEADS // 2, P])
        rden = sb("rden", [P, HEADS])
        att = sb("att", [P, D])
        oT0 = sb("oT0", [P, P])
        oT1 = sb("oT1", [D1 + 1, P])
        st2 = sb("st2", [P, 6])
        mv2 = sb("mv2", [P, 2])
        ve2 = sb("ve2", [P, 1])
        rstd2 = sb("rstd2", [P, 1])
        x2 = sb("x2", [P, 2, D])
        rows = sb("rows", [P, 4, ROW])
        x2T0 = sb("x2T0", [P, P])
        x2T1 = sb("x2T1", [D1, P])
        squares = sb("squares", [P, D])
        ssq = sb("ssq", [P, 2])
        ms = sb("ms", [P, 2])
        lg = sb("lg", [P, E])
        top = sb("top", [P, 2, E])
        choice = sb("choice", [P, 2, E], U32)
        chosen = sb("chosen", [P, 4])
        hot = sb("hot", [P, 2, 2, E])
        hots = sb("hots", [P, 2, E], BF16)
        count = sb("count", [P, E])
        pos = sb("pos", [P, 2, E])
        posk = sb("posk", [P, 2, 2, E])
        pk = sb("pk", [P, 4])
        base = sb("base", [P, 4])
        over = sb("over", [P, 4])
        gapd = sb("gapd", [P, 2])
        ratio = sb("ratio", [P, 2])
        total = sb("total", [P, 2])
        wts = sb("wts", [P, 2, 2])
        wk = sb("wk", [P, 2, 2, E])
        slot = sb("slot", [P, 2, 4], U32)
        rawa_sb = sb("rawa_sb", [P, 2 * H])
        rawb_sb = sb("rawb_sb", [P, 2 * H])
        wah = sb("wah", [P, 2, 2 * H], F32R)
        wal = sb("wal", [P, 2, 2 * H], F32R)
        wbh = sb("wbh", [P, 2, 2 * H], F32R)
        wbl = sb("wbl", [D1, 2, 2 * H], F32R)
        w2_sb = sb("w2_sb", [P, 2, MH, D])
        nw0_sb = sb("nw0_sb", [P, E])
        nw1_sb = sb("nw1_sb", [P, E])
        zs = sb("zs", [CR, 2, CC, ROW])
        zn0 = sb("zn0", [CR, CC, D0])
        zn1 = sb("zn1", [CR, CC, 2, D1])
        z0h = sb("z0h", [P, 2, CAP], F32R)
        z0l = sb("z0l", [P, 2, CAP], F32R)
        z1 = sb("z1", [P, 2, CAP], F32R)
        sg = sb("sg", [P, 2, CAP])
        hT = sb("hT", [P, MH, CAP])
        yx = sb("yx", [CR, CC, D])
        yw = sb("yw", [CR, CC, D])
        tok = sb("tok", [CR, E, CC], U32)

        bank = [ctx.enter_context(nc.psum_tensor(f"bank{i}", [P, 512], F32)) for i in range(8)]

        s_patch = sem("patch_in"); s_tokw = sem("tokw_in"); s_posb = sem("posb_in")
        s_const = sem("const_in"); s_wqkv = sem("wqkv_in"); s_wo = sem("wo_in")
        s_txt = sem("txt_in"); s_small = sem("small_in")
        s_patch_rest = sem("other_patches_in"); s_ptok_in = [sem("patch_tokens_placed_tile0"), sem("patch_tokens_placed_tiles1to3")]
        s_fused = sem("other_patch_tokens_out"); s_fused_in = sem("other_patch_tokens_placed"); s_h_out = sem("h_out")
        s_zero = sem("zero_ready"); s_gaps = sem("gaps_ready"); s_ones = sem("ones_ready")
        s_pe_tok = sem("patch_product"); s_posum = sem("pos_bias_sum"); s_ptok = sem("patch_tokens_ready")
        s_order = sem("order_bf16"); s_stat = sem("stats_ready"); s_rstd1 = sem("rstd1_ready")
        s_idle = sem("idle_operand_ready"); s_pre = sem("vector_pre_step"); s_stats = sem("statistics1"); s_zeroed = sem("rows_zeroed")
        s_xn = sem("xn_ready"); s_xt = sem("xn_turned"); s_xT = sem("xT_ready")
        s_qkv = sem("qk_product"); s_vp = sem("v_product"); s_rope = sem("rope_parts"); s_qk = sem("qk_ready")
        s_v = sem("v_ready"); s_qkt = sem("qk_turned"); s_qkT = sem("qkT_ready")
        sA = sem("vector_step_A")
        s_sc = sem("scores"); s_sh = sem("scores_shifted"); s_exp = sem("exp_ready")
        s_pt = sem("probs_turned"); s_pT = sem("pT_ready"); s_mx = sem("maximum_ready")
        s_scread = sem("scores_read")
        s_pv = sem("values_product"); s_att = sem("attention_ready"); s_ot = sem("attention_turned")
        s_oT = sem("oT_ready"); s_proj = sem("projection"); s_var2 = sem("variance2_ready")
        s_rstd2 = sem("rstd2_ready"); s_x2 = sem("x2_ready"); sC = sem("vector_step_C")
        s_res = sem("residual_added"); s_st2 = sem("statistics2"); s_mv2 = sem("mean_variance2")
        s_x2t = sem("x2_turned"); s_x2T = sem("x2T_ready"); s_ssq = sem("square_sum")
        s_ms = sem("mean_square"); s_rms = sem("rms_ready"); s_gate = sem("logits")
        s_lg = sem("logits_copied"); s_top = sem("logits_sorted"); s_choice = sem("choice_ready")
        s_chosen = sem("chosen_ready"); s_diff = sem("logit_gap"); s_ratio = sem("ratio_ready")
        s_hots = sem("hots_ready"); s_pos = sem("positions"); s_slot = sem("slot_ready")
        s_disp = sem("slots_written"); sR1 = sem("vector_step_R1")
        sR2 = sem("vector_step_R2"); s_rowx = sem("row_x_ready")
        s_raw = sem("w13_in"); s_w2 = [sem("w2_in_even"), sem("w2_in_odd")]; s_nw = sem("norm_w_in")
        s_zs = [sem("slots_in_even"), sem("slots_in_odd")]
        s_zn = sem("z_scaled"); s_zt = sem("z_turned"); s_zh = sem("z_high"); s_z = sem("z_ready")
        s_wh = sem("weights_high"); s_wl = sem("weights_rest")
        s_up = sem("up_product"); s_silu = sem("silu_ready"); s_hT = sem("hidden_ready")
        s_down = sem("down_product"); s_yx = sem("y_plus_x"); s_yw = sem("y_weighted")
        s_tok = sem("token_index"); s_add = sem("added")

        block = ctx.enter_context(nc.Block())

        def pipeline(eng, iteration):
            def stages(i):
                return ([0 <= i - k < NT for k in range(5)]
                        + [i % 2 == 1 and 5 <= i <= NT + 3, i % 2 == 0 and 6 <= i <= NT + 4])

            for i in range(PEEL):
                iteration(i, i // 2, i, i % 4, *stages(i))
            with eng.Fori(PEEL // 4, NT // 4 - 1) as turn:
                for k in range(PEEL, PEEL + 4):
                    iteration(turn * 4 + (k - 4), turn * 2 + (k // 2 - 2), PEEL, k % 4, *stages(k))
            for i in range(NT - 2, NT + 5):
                iteration(i, i // 2, i, i % 4, *stages(i))

        @block.sync
        def _(sp):
            sp.dma_start(tokw_sb[:, :, :], tokw).then_inc(s_tokw, 16)
            sp.dma_start(patch_sb[:, :, 0:P], patches[:, :, 0:P]).then_inc(s_patch, 16)
            sp.dma_start(posb_sb[:, :], posb).then_inc(s_posb, 16)
            sp.dma_start(tokb_sb[:, :], tokb).then_inc(s_posb, 16)
            sp.dma_start(small_sb[:, :], small).then_inc(s_small, 16)
            sp.dma_start(patch_sb[:, :, P:4 * P], patches[:, :, P:4 * P]).then_inc(s_patch_rest, 16)
            sp.dma_start(ident_sb[:, :], ident).then_inc(s_const, 16)
            sp.dma_start(wqkv0_sb[:, :], wqkv[0:P, :]).then_inc(s_wqkv, 16)
            sp.dma_start(wqkv1_sb[:, :], wqkv[P:D + 1, :]).then_inc(s_wqkv, 16)
            sp.wait_ge(s_gaps, 2)
            tx = txt.rearrange("(t two) s d -> two s t d", two=2)
            for two in range(2):
                at = two * HALF + NPATCH
                sp.dma_start(h_all[at:at + NTXT, :, :], tx[two]).then_inc(s_txt, 16)
            sp.dma_start(rope_sb[:, :, :], rope.rearrange("p (a b) -> p a b", a=2)).then_inc(s_const, 16)
            sp.dma_start(mask_sb[:, :, :], mask.rearrange("p (a b) -> p a b", a=HEADS)).then_inc(s_const, 16)
            sp.dma_start(orderf_sb[:, :], order).then_inc(s_const, 16)
            sp.dma_start(wo0_sb[:, :], wo[0:P, :]).then_inc(s_wo, 16)
            sp.dma_start(wo1_sb[:, :], wo[P:D + 1, :]).then_inc(s_wo, 16)
            sp.dma_start(gate_sb[:, 0, :], gate[0:P, :]).then_inc(s_wo, 16)
            sp.dma_start(gate_sb[0:D1, 1, :], gate[P:D, :]).then_inc(s_wo, 16)
            sp.wait_ge(s_ptok, 4)
            sp.dma_start(fused.rearrange("(g p) d -> p g d", p=P), ptok_sb[:, 1:4, :]).then_inc(s_fused, 16)
            sp.wait_ge(s_fused, 16)
            fu = fused.rearrange("(t two s) d -> two s t d", two=2, s=NPATCH)
            for two in range(2):
                sp.dma_start(h_all[two * HALF:two * HALF + NPATCH, 4:NT, :], fu[two]).then_inc(s_fused_in, 16)
            sp.wait_ge(s_zero, 1)
            sp.dma_start(out[N:N + CAP, :].rearrange("(c p) d -> p c d", p=CR),
                         zero_sb[0:CR, 0:CC, 0:D]).then_inc(s_h_out, 16)
            sp.dma_start(nw0_sb[:, :], normw[0:P, :]).then_inc(s_nw, 16)
            for lo in (0, D1):
                sp.dma_start(nw1_sb[lo:lo + D1, :], normw[P:D, :]).then_inc(s_nw, 16)

            def load_w13(e):
                sp.dma_start(rawa_sb[:, :], w13[bass.ds(e * D, P), :]).then_inc(s_raw, 16)
                for lo in (0, D1):
                    sp.dma_start(rawb_sb[lo:lo + D1, :], w13[bass.ds(e * D + P, D1), :]).then_inc(s_raw, 16)

            def load_w2(e, par):
                sp.dma_start(w2_sb[:, par, :, :],
                             w2[bass.ds(e * H, H), :].rearrange("(m p) d -> p m d", p=P)).then_inc(s_w2[par], 16)

            def load_slots(e, par):
                sp.dma_start(zs[:, par, :, :],
                             slots[bass.ds(e * CAP, CAP), :].rearrange("(c p) r -> p c r", p=CR)).then_inc(s_zs[par], 16)

            load_w13(0)
            load_w2(0, 0)
            load_w2(1, 1)
            ho = out[0:N, :].rearrange("(b s) d -> b s d", s=S).rearrange("(t two) s d -> two s t d", two=2)

            def residual(tiles):
                sp.wait_ge(s_x2, tiles.stop)
                for two in range(2):
                    sp.dma_start(ho[two, :, tiles], h_all[two * HALF:two * HALF + S, tiles, :]).then_inc(s_h_out, 16)

            residual(slice(0, NT - 4))
            sp.wait_ge(s_disp, 32 * NT + 16)
            load_slots(0, 0)
            load_slots(1, 1)
            residual(slice(NT - 4, NT))
            sp.wait_ge(s_wl, 2)
            load_w13(1)
            with sp.Fori(1, E // 2) as pair:
                for par in range(2):
                    e = pair * 2
                    sp.wait_ge(s_wl, 2 * (e + par))
                    load_w13(e + par)
                    sp.wait_ge(s_down, 2 * (e + (par - 1)))
                    load_w2(e + par, par)
                    sp.wait_ge(s_yw, CC * (e + (par - 1)))
                    sp.wait_ge(s_tok, e + (par - 1))
                    load_slots(e + par, par)

        @block.tensor
        def _(pe):
            def stay_warm(n):
                for _ in range(n):
                    pe.matmul(bank[0][:, :], idle_sb[:, 0:P], idle_sb[:, :], start=True, stop=True)

            pe.wait_ge(s_idle, 1)
            stay_warm(11)
            pe.wait_ge(s_tokw, 16)
            pe.wait_ge(s_patch, 16)
            for g in range(4):
                if g == 1:
                    pe.wait_ge(s_patch_rest, 16)
                for k in range(PK):
                    mm = pe.matmul(bank[g][:, 0:D], patch_sb[:, k, g * P:(g + 1) * P], tokw_sb[:, k, :],
                                   start=(k == 0), stop=(k == PK - 1))
                mm.then_inc(s_pe_tok, 1)
            pe.wait_ge(s_const, 16 * 4)
            pe.wait_ge(s_wqkv, 32)
            pe.wait_ge(s_wo, 64)
            pe.wait_ge(s_ones, 1)
            pe.wait_ge(s_ptok, 4)

            def iteration(i, half, i0, quad, a, b, c, d, m, r1, r2):
                par = quad % 2
                if a:
                    pe.wait_ge(s_xn, i + 1)
                    if i0 >= 1:
                        pe.wait_ge(s_rope, i)
                    pe.transpose(bank[4][:, 0:P], xn[:, 0:D0], ident_sb[:, :])
                    pe.transpose(bank[4][0:D1, P:2 * P], xn[:, D0:D], ident_sb[:, :]).then_inc(s_xt, 1)
                if c:
                    pe.wait_ge(s_pT, 2 * (i - 1))
                    pe.wait_ge(s_v, 4 * (i - 1))
                    if i0 >= 3:
                        pe.wait_ge(s_res, i - 2)
                    for p in range(HEADS // 2):
                        for two in range(2):
                            lo = two * HALF
                            w = 2 * (HD + 1)
                            mm = pe.matmul(bank[6][lo:lo + HALF, p * w:(p + 1) * w],
                                           pT[:, par, p, lo:lo + HALF],
                                           vbd[:, par, two, p, :, :].rearrange("p a b -> p (a b)"),
                                           start=True, stop=True)
                    mm.then_inc(s_pv, 1)
                if b:
                    pe.wait_ge(s_qkT, 5 * i)
                    if i0 >= 2:
                        pe.wait_ge(s_pT, 2 * (i - 1))
                    q = 1 - par
                    for g in range(HG):
                        for two in range(2):
                            lo = two * HALF
                            mm = pe.matmul(bank[g // 2][lo:lo + HALF, (g % 2) * 4 * S:(g % 2 + 1) * 4 * S],
                                           qT[:, q, g, lo:lo + HALF],
                                           kbd[:, q, two, g, :, :].rearrange("p a b -> p (a b)"),
                                           start=True, stop=True)
                    mm.then_inc(s_sc, 1)
                if c:
                    pe.wait_ge(s_att, i - 1)
                    pe.transpose(bank[6][:, 0:P], att[:, 0:D0], ident_sb[:, :])
                    pe.transpose(bank[6][0:D1, P:2 * P], att[:, D0:D], ident_sb[:, :]).then_inc(s_ot, 1)
                if a:
                    pe.wait_ge(s_xT, i + 1)
                    pe.matmul(bank[4][:, 0:2 * D], xT0[:, :], wqkv0_sb[:, 0:2 * D], start=True, stop=False)
                    pe.matmul(bank[4][:, 0:2 * D], xT1[:, :], wqkv1_sb[:, 0:2 * D], start=False, stop=True).then_inc(s_qkv, 1)
                    if i0 >= 1:
                        pe.wait_ge(s_v, 4 * i)
                    pe.matmul(bank[5][:, 0:D], xT0[:, :], wqkv0_sb[:, 2 * D:3 * D], start=True, stop=False)
                    pe.matmul(bank[5][:, 0:D], xT1[:, :], wqkv1_sb[:, 2 * D:3 * D], start=False, stop=True).then_inc(s_vp, 1)
                if c:
                    pe.wait_ge(s_oT, i - 1)
                    pe.matmul(bank[6][:, 0:D], oT0[:, :], wo0_sb[:, :], start=True, stop=False)
                    pe.matmul(bank[6][:, 0:D], oT1[:, :], wo1_sb[:, :], start=False, stop=True).then_inc(s_proj, 1)
                if d:
                    pe.wait_ge(s_x2, i - 2)
                    if i0 >= 4:
                        pe.wait_ge(s_lg, i - 3)
                    if i0 >= 6 and not par:
                        pe.wait_ge(sR2, STEPS["R2"] * (half - 3) + 2)
                    pe.transpose(bank[7][:, 0:P], x2[:, 1 - par, 0:D0], ident_sb[:, :])
                    pe.transpose(bank[7][0:D1, P:2 * P], x2[:, 1 - par, D0:D], ident_sb[:, :]).then_inc(s_x2t, 1)
                if b:
                    pe.wait_ge(s_exp, i)
                    for p in range(HEADS // 2):
                        mm = pe.transpose(bank[p // 3][:, (p % 3) * P:(p % 3 + 1) * P],
                                          pr[:, 2 * p:2 * p + 2, :].rearrange("p a b -> p (a b)"), ident_sb[:, :])
                        if p % 3 == 2:
                            mm.then_inc(s_pt, 1)
                if a:
                    for r in (1, 0):
                        pe.wait_ge(s_qk, 2 * i + 2 - r)
                        for g in range(HG):
                            mm = pe.transpose(bank[2 + r][:, g * P:(g + 1) * P],
                                              qk[:, r, 4 * g:4 * g + 4, :].rearrange("p a b -> p (a b)"), ident_sb[:, :])
                        mm.then_inc(s_qkt, 1)
                if d:
                    pe.wait_ge(s_x2T, i - 2)
                elif r1:
                    pe.wait_ge(s_lg, i - 3)
                if r1:
                    pe.wait_ge(s_hots, half - 1)
                    p0 = 2 * P
                    pe.matmul(bank[7][:, p0:p0 + E], order_sb[:, 0:P], hots[:, 0, :], start=True, stop=True)
                    pe.matmul(bank[7][:, p0 + E:p0 + 2 * E], order_sb[:, 0:P], hots[:, 1, :], start=True, stop=False)
                    pe.matmul(bank[7][:, p0 + E:p0 + 2 * E], order_sb[:, P:2 * P], hots[:, 0, :], start=False, stop=True)
                    pe.matmul(bank[7][:, p0 + 2 * E:p0 + 3 * E], order_sb[:, P:2 * P], hots[:, 0, :], start=True, stop=False)
                    pe.matmul(bank[7][:, p0 + 2 * E:p0 + 3 * E], order_sb[:, P:2 * P], hots[:, 1, :],
                              start=False, stop=True).then_inc(s_pos, 1)
                if d:
                    pe.matmul(bank[7][:, 0:E], x2T0[:, :], gate_sb[:, 0, :], start=True, stop=False)
                    pe.matmul(bank[7][:, 0:E], x2T1[:, :], gate_sb[0:D1, 1, :], start=False, stop=True).then_inc(s_gate, 1)

            pipeline(pe, iteration)

            def turn(e, par):
                for n, (zn, wide) in enumerate(((zn0, "c d -> c d"), (zn1, "c a d -> c (a d)"))):
                    pe.wait_ge(s_zn, 2 * e + (n + 1))
                    for c in range(CC):
                        mm = pe.transpose(bank[4 + n][:, c * CR:(c + 1) * CR], zn[:, c].rearrange(wide),
                                          ident_sb[0:CR, 0:CR])
                    mm.then_inc(s_zt, 1)

            def expert(e, e0, par, more):
                pe.wait_ge(s_wl, 2 * (e + 1))
                pe.wait_ge(s_zh, 2 * e + 1)
                for m in range(MH):
                    q = 2 * (m % 2)
                    if e0 >= 1 or m >= 2:
                        pe.wait_ge(s_hT, MH * e + m - 1)
                    for r in range(2):
                        cols = slice(r * H + m * P, r * H + (m + 1) * P)
                        o = bank[q + r][:, 0:CAP]
                        pe.matmul(o, wah[:, par, cols], z0h[:, par, :], start=True, stop=False)
                        pe.matmul(o, wal[:, par, cols], z0h[:, par, :], start=False, stop=False)
                        if m == 0 and r == 0:
                            pe.wait_ge(s_z, 2 * e + 1)
                        pe.matmul(o, wah[:, par, cols], z0l[:, par, :], start=False, stop=False)
                        if m == 0 and r == 0:
                            pe.wait_ge(s_z, 2 * e + 2)
                        pe.matmul(o, wbh[:, par, cols], z1[:, par, :], start=False, stop=False)
                        mm = pe.matmul(o, wbl[:, par, cols], z1[0:D1, par, :], start=False, stop=True)
                    mm.then_inc(s_up, 1)
                if more:
                    turn(e + 1, 1 - par)
                pe.wait_ge(s_w2[par], 8 * (e - par) + 16)
                for c, parts in ((0, (0, 1, 2)), (2, (0, 1, 2)), (0, (3,)), (2, (3,)),
                                 (1, (0, 1, 2, 3)), (3, (0, 1, 2, 3))):
                    if parts[0] == 0 and c == 0:
                        pe.wait_ge(s_hT, MH * e + 3)
                    if parts[0] == 3 and c == 0:
                        pe.wait_ge(s_hT, MH * (e + 1))
                    if parts[0] == 0 and c % 2 == 0 and e0 >= 1:
                        pe.wait_ge(s_yx, 2 * e + (c // 2 - 1))
                    for m in parts:
                        mm = pe.matmul(bank[6 + c // 2][0:CR, (c % 2) * D:(c % 2 + 1) * D],
                                       hT[:, m, c * CR:(c + 1) * CR], w2_sb[:, par, m, :],
                                       start=(m == 0), stop=(m == MH - 1))
                    if c % 2 == 1:
                        mm.then_inc(s_down, 1)

            pe.wait_ge(s_slot, NT // 2)
            stay_warm(34)
            turn(0, 0)
            expert(0, 0, 0, True)
            expert(1, 1, 1, True)
            with pe.Fori(1, E // 2 - 1) as pair:
                expert(pair * 2, 2, 0, True)
                expert(pair * 2 + 1, 3, 1, True)
            expert(E - 2, E - 2, 0, True)
            expert(E - 1, E - 1, 1, False)

        @block.scalar
        def _(act):
            act.wait_ge(s_gaps, 2)
            act.wait_ge(s_ptok, 1)
            for j in range(P // NPATCH):
                at = (j % 2) * HALF
                act.dma_start(h_all[at:at + NPATCH, j // 2, :],
                              ptok_sb[j * NPATCH:(j + 1) * NPATCH, 0, :]).then_inc(s_ptok_in[j > 1], 16)
            act.wait_ge(s_ones, 1)

            def iteration(i, half, i0, quad, a, b, c, d, m, r1, r2):
                par = quad % 2
                if a:
                    act.wait_ge(s_xt, i + 1)
                    if i0 >= 1:
                        act.wait_ge(s_vp, i)
                    act.copy(xT0[:, :], bank[4][:, 0:P])
                    act.copy(xT1[0:D1, :], bank[4][0:D1, P:2 * P]).then_inc(s_xT, 1)
                if c:
                    act.wait_ge(s_ot, i - 1)
                    if i0 >= 3:
                        act.wait_ge(s_proj, i - 2)
                    act.copy(oT0[:, :], bank[6][:, 0:P])
                    act.copy(oT1[0:D1, :], bank[6][0:D1, P:2 * P]).then_inc(s_oT, 1)
                if b:
                    act.wait_ge(s_sh, i)
                    if i0 >= 2:
                        act.wait_ge(s_pt, 2 * (i - 1))
                    act.activation(pr[:, :, 0:S], sm[:, :].rearrange("p (h k) -> p h k", k=S), ACT.Exp).then_inc(s_exp, 1)
                if d:
                    act.wait_ge(s_x2t, i - 2)
                    if i0 >= 4:
                        act.wait_ge(s_gate, i - 3)
                    act.copy(x2T0[:, :], bank[7][:, 0:P])
                    act.copy(x2T1[:, :], bank[7][0:D1, P:2 * P]).then_inc(s_x2T, 1)
                if b:
                    for r in range(2):
                        act.wait_ge(s_pt, 2 * (i - 1) + r + 1)
                        if r == 0 and i0 >= 3:
                            act.wait_ge(s_pv, i - 2)
                        act.copy(pT[:, 1 - par, 3 * r:3 * r + 3, :].rearrange("p a b -> p (a b)"),
                                 bank[r][:, 0:3 * P]).then_inc(s_pT, 1)
                if r1:
                    act.wait_ge(s_diff, half - 1)
                    if i0 >= 6:
                        act.wait_ge(sR2, STEPS["R2"] * (half - 2))
                    act.activation(ratio[:, :], gapd[:, :], ACT.Exp).then_inc(s_ratio, 1)
                if d:
                    act.wait_ge(s_x2, i - 2)
                    if i0 >= 5:
                        act.wait_ge(s_ms, i - 4)
                    act.activation(squares[:, :], x2[:, 1 - par, :], ACT.Square, scale=D ** -0.5,
                                   accum_out=ssq[:, 1 - par:2 - par]).then_inc(s_ssq, 1)
                    if i0 >= 6:
                        act.wait_ge(s_disp, 32 * (i - 6) + 16)
                    act.copy(rows[:, (quad + 1) % 4, 0:D],
                             x2[:, 1 - par, :]).then_inc(s_rowx, 1)
                if a:
                    act.wait_ge(s_qkt, 2 * i + 1)
                    if i0 >= 2:
                        act.wait_ge(s_sc, i - 1)
                    for j in range(4):
                        rows_k = bank[3][32 * j:32 * j + 32, 0:3 * P].rearrange("p (g two k) -> p two g k", g=HG, two=2)
                        act.copy(kbd[32 * j:32 * j + 32, par, :, :, j, :], rows_k[:, :, :, 0:S]).then_inc(s_qkT, 1)
                    act.wait_ge(s_qkt, 2 * i + 2)
                    act.copy(qT[:, par, :, :].rearrange("p a b -> p (a b)"), bank[2][:, 0:3 * P]).then_inc(s_qkT, 1)
                if a:
                    act.wait_ge(s_vp, i + 1)
                    if i0 >= 2:
                        act.wait_ge(s_pv, i - 1)
                    for two in range(2):
                        for odd in range(2):
                            row, lo = two * HALF, odd * HALF
                            act.copy(vbd[lo:lo + HALF, par, two, :, odd, 0:HD],
                                     bank[5][row:row + HALF, 0:D].rearrange(
                                         "p (a b d) -> p a b d", b=2, d=HD)[:, :, odd, :]).then_inc(s_v, 1)

            pipeline(act, iteration)

            def prepare(e, e0, par):
                act.wait_ge(s_zt, 2 * e + 1)
                if e0 >= 2:
                    act.wait_ge(s_up, MH * (e - 1))
                act.mul(z0h[:, par, :], bank[4][:, 0:CAP], nw0_sb[:, bass.ds(e, 1)]).then_inc(s_zh, 1)
                act.wait_ge(s_zt, 2 * e + 2)
                act.mul(z1[:, par, :], bank[5][:, 0:CAP], nw1_sb[:, bass.ds(e, 1)]).then_inc(s_zh, 1)

            def split_high(e, e0, par, n):
                if n == 0:
                    act.wait_ge(s_raw, 48 * (e + 1))
                act.copy((wah, wbh)[n][:, par, :], (rawa_sb, rawb_sb)[n][:, :]).then_inc(s_wh, 1)

            def expert(e, e0, par, more):
                for m in range(MH):
                    act.wait_ge(s_up, MH * e + m + 1)
                    if e0 >= 1 or m >= 2:
                        act.wait_ge(s_hT, MH * e + m - 1)
                    act.activation(sg[:, m % 2, :], bank[2 * (m % 2)][:, 0:CAP], ACT.Silu).then_inc(s_silu, 1)
                    if more and m < 2:
                        split_high(e + 1, e0 + 1, 1 - par, m)
                if more:
                    prepare(e + 1, e0 + 1, 1 - par)
                for c in range(CC):
                    act.wait_ge(s_yx, 2 * e + c // 2 + 1)
                    if e0 >= 1 and c == 0:
                        act.wait_ge(s_add, 64 * e)
                    act.mul(yw[:, c, :], yx[:, c, :], zs[:, par, c, bass.ds(e + W_COL, 1)]).then_inc(s_yw, 1)

            act.wait_ge(s_nw, 48)
            for n in range(2):
                split_high(0, 0, 0, n)
            prepare(0, 0, 0)
            expert(0, 0, 0, True)
            expert(1, 1, 1, True)
            with act.Fori(1, E // 2 - 1) as pair:
                expert(pair * 2, 2, 0, True)
                expert(pair * 2 + 1, 3, 1, True)
            expert(E - 2, E - 2, 0, True)
            expert(E - 1, E - 1, 1, False)

        @block.vector
        def _(dve):
            dve.memset(idle_sb[:, :], 0.0).then_inc(s_idle, 1)
            dve.memset(xT1[D1:D1 + 1, :], 1.0)
            dve.memset(oT1[D1:D1 + 1, :], 1.0)
            dve.memset(qk[:, :, :, :], 0.0)
            dve.memset(vbd[:, :, :, :, :, :], 0.0).then_inc(s_pre, 1)
            dve.wait_ge(s_pre, 1)
            dve.memset(vbd[0:HALF, :, :, :, 0, HD:HD + 1], 1.0)
            dve.memset(vbd[HALF:P, :, :, :, 1, HD:HD + 1], 1.0)
            dve.wait_ge(s_posb, 32)
            dve.tensor_tensor(posb_sb[:, :], posb_sb[:, :], tokb_sb[:, :], ALU.add).then_inc(s_posum, 1)
            dve.wait_ge(s_posum, 1)

            def patch_tokens(g):
                dve.wait_ge(s_pe_tok, g + 1)
                dve.tensor_tensor(ptok_sb[:, g, :], bank[g][:, 0:D], posb_sb[:, :], ALU.add).then_inc(s_ptok, 1)

            def statistics(g):
                lo, hi = STAT_TILES[g]
                if g < 2:
                    dve.wait_ge(s_ptok_in[g], 16 * 2 * (hi - lo))
                if g == 2:
                    dve.wait_ge(s_fused_in, 32)
                for t in range(lo, hi):
                    ins = dve.bn_stats(stats[:, t, :], h_all[:, t, :])
                ins.then_inc(s_stats, 1)
                dve.wait_ge(s_stats, 2 * g + 1)
                for t in range(lo, hi):
                    ins = dve.bn_aggr(mv[:, t, :], stats[:, t, :])
                ins.then_inc(s_stats, 1)
                dve.wait_ge(s_stats, 2 * g + 2)
                dve.tensor_scalar(ve1[:, lo:hi], mv[:, lo:hi, 1], LN_EPS, None, ALU.add).then_inc(s_stat, 1)

            patch_tokens(0)
            dve.memset(pr[:, :, :], 0.0)
            dve.memset(count[:, :], 0.0)
            patch_tokens(1)
            dve.memset(kbd[:, :, :, :, :, :], 0.0).then_inc(s_ones, 1)
            dve.wait_ge(s_gaps, 2)
            dve.wait_ge(s_txt, 32)
            statistics(0)
            patch_tokens(2)
            patch_tokens(3)
            dve.wait_ge(s_rstd1, 1)

            def norm1(t, t0):
                if t0 >= 1:
                    dve.wait_ge(s_xt, t)
                dve.tensor_scalar(xn[:, :], h_all[:, bass.ds(t, 1), :].rearrange("p a d -> p (a d)"),
                                  mv[:, bass.ds(t, 1), 0], rstd1[:, bass.ds(t, 1)],
                                  ALU.subtract, ALU.mult).then_inc(s_xn, 1)

            def steps(sem_, name, t):
                k = [0]

                def link(ins, wait=True):
                    k[0] += 1
                    ins.then_inc(sem_, 1)
                    if wait:
                        dve.wait_ge(sem_, STEPS[name] * t + k[0])

                def done():
                    assert k[0] == STEPS[name], (name, k[0])
                return link, done

            norm1(0, 0)
            statistics(1)
            dve.wait_ge(s_const, 16 * 4)
            dve.tensor_copy(order_sb[:, :], orderf_sb[:, :]).then_inc(s_order, 1)

            def iteration(i, half, i0, quad, a, b, c, d, m, r1, r2):
                par = quad % 2
                if m:
                    dve.wait_ge(s_gate, i - 3)
                    dve.tensor_copy(lg[:, :], bank[7][:, 0:E]).then_inc(s_lg, 1)
                if m:
                    q = par
                    dve.wait_ge(s_ones, 1)
                    dve.wait_ge(s_lg, i - 3)
                    dve.max(top[:, q, :], lg[:, :]).then_inc(s_top, 1)
                    dve.wait_ge(s_ones, 1)
                    dve.wait_ge(s_top, i - 3)
                    dve.max_index(choice[:, q, :], top[:, q, :], lg[:, :]).then_inc(s_choice, 1)
                    dve.wait_ge(s_choice, i - 3)
                    dve.tensor_copy(chosen[:, 2 * q:2 * q + 2], choice[:, q, 0:2]).then_inc(s_chosen, 1)
                    if r1:
                        dve.wait_ge(s_chosen, i - 3)
                if r2:
                    link_r2, done_r2 = steps(sR2, "R2", half - 3)
                    dve.wait_ge(s_pos, half - 2)
                    p0 = 2 * P
                    link_r2(dve.tensor_tensor(pos[:, :, :], bank[7][:, p0:p0 + 2 * E].rearrange("p (a e) -> p a e", a=2),
                                              count[:, :].unsqueeze(1).to_broadcast([P, 2, E]), ALU.add))
                    link_r2(dve.tensor_tensor(count[:, :], bank[7][:, p0 + 2 * E:p0 + 3 * E], count[:, :], ALU.add),
                            wait=False)
                if c:
                    link, done = steps(sC, "C", i - 2)
                    dve.wait_ge(s_pv, i - 1)
                    o4 = bank[6][:, 0:HEADS * (HD + 1)].rearrange("p (h d) -> p h d", h=HEADS)
                    link(dve.reciprocal(rden[:, :], o4[:, :, HD]))
                    if i0 >= 3:
                        dve.wait_ge(s_ot, i - 2)
                    dve.tensor_tensor(att[:, :].rearrange("p (h d) -> p h d", h=HEADS), o4[:, :, 0:HD],
                                      rden[:, :].unsqueeze(2).to_broadcast([P, HEADS, HD]),
                                      ALU.mult).then_inc(s_att, 1)
                if d:
                    dve.wait_ge(s_rstd2, i - 2)
                    if i0 >= 5:
                        dve.wait_ge(s_rowx, i - 4)
                        dve.wait_ge(s_x2t, i - 4)
                    dve.tensor_scalar(x2[:, 1 - par, :], h_all[:, bass.ds(i - 3, 1), :].rearrange("p a d -> p (a d)"),
                                      mv2[:, 0:1], rstd2[:, :], ALU.subtract, ALU.mult).then_inc(s_x2, 1)
                if b:
                    dve.wait_ge(s_sc, i)
                    if i0 >= 2:
                        dve.wait_ge(s_exp, i - 1)
                    dve.tensor_tensor(sm[:, 0:8 * S], bank[0][:, 0:8 * S],
                                      mask_sb[:, 0:8, :].rearrange("p a b -> p (a b)"), ALU.add)
                    dve.tensor_tensor(sm[:, 8 * S:12 * S], bank[1][:, 0:4 * S],
                                      mask_sb[:, 8:12, :].rearrange("p a b -> p (a b)"), ALU.add).then_inc(s_scread, 1)
                    dve.wait_ge(s_scread, i)
                    sm3 = sm[:, :].rearrange("p (h k) -> p h k", k=S)
                    dve.tensor_reduce(mx[:, :], sm3, AX.X, ALU.max).then_inc(s_mx, 1)
                if b:
                    dve.wait_ge(s_mx, i)
                    sm3 = sm[:, :].rearrange("p (h k) -> p h k", k=S)
                    dve.tensor_tensor(sm3, sm3, mx[:, :].unsqueeze(2).to_broadcast([P, HEADS, S]),
                                      ALU.subtract).then_inc(s_sh, 1)
                if a:
                    dve.wait_ge(s_qkv, i + 1)
                    if i0 >= 1:
                        dve.wait_ge(s_qk, 2 * i)
                    q2 = bank[4][:, 0:2 * D]
                    dve.tensor_tensor(rc[:, :], q2, rope_sb[:, 0, :], ALU.mult)
                    pairs = q2.rearrange("p (n two) -> p n two", two=2)
                    rs2 = rs[:, :].rearrange("p (n two) -> p n two", two=2)
                    sn2 = rope_sb[:, 1, :].rearrange("p (n two) -> p n two", two=2)
                    dve.tensor_tensor(rs2[:, :, 0], pairs[:, :, 1], sn2[:, :, 0], ALU.mult)
                    dve.tensor_tensor(rs2[:, :, 1], pairs[:, :, 0], sn2[:, :, 1], ALU.mult).then_inc(s_rope, 1)
                if r1:
                    link, done = steps(sR1, "R1", half - 2)
                    dve.tensor_tensor(gapd[:, :], top[:, :, 1], top[:, :, 0], ALU.subtract).then_inc(s_diff, 1)
                    ex = small_sb[:, EXP0:EXP0 + E].unsqueeze(1).to_broadcast([P, 4, E])
                    link(dve.tensor_tensor(hot[:, :, :, :].rearrange("p a b e -> p (a b) e"), ex,
                                           chosen[:, :].unsqueeze(2).to_broadcast([P, 4, E]), ALU.is_equal))
                    dve.tensor_tensor(hots[:, :, :], hot[:, :, 0, :], hot[:, :, 1, :], ALU.add).then_inc(s_hots, 1)
                    link(dve.tensor_scalar(base[:, :], chosen[:, :], float(CAP), small_sb[:, GAP0:GAP0 + 1],
                                           ALU.mult, ALU.add), wait=False)
                    done()
                if a and i0 + 1 < NT:
                    if i0 == 0:
                        dve.wait_ge(s_rstd1, 2)
                    if i0 in (3, 5):
                        dve.wait_ge(s_rstd1, i0)
                    norm1(i + 1, i0 + 1)
                if r2:
                    link, done = link_r2, done_r2
                    dve.wait_ge(sR2, STEPS["R2"] * (half - 3) + 2)
                    dve.tensor_tensor(posk[:, :, :, :], hot[:, :, :, :],
                                      pos[:, :, :].unsqueeze(2).to_broadcast([P, 2, 2, E]), ALU.mult)
                    dve.wait_ge(s_ratio, half - 2)
                    link(dve.tensor_scalar(total[:, :], ratio[:, :], 1.0, None, ALU.add))
                    link(dve.tensor_reduce(pk[:, :], posk[:, :, :, :].rearrange("p a b e -> p (a b) e"), AX.X, ALU.add),
                         wait=False)
                    link(dve.reciprocal(wts[:, :, 0], total[:, :]))
                    link(dve.tensor_tensor(base[:, :], base[:, :], pk[:, :], ALU.add), wait=False)
                    dve.tensor_tensor(wts[:, :, 1], wts[:, :, 0], ratio[:, :], ALU.mult)
                    link(dve.tensor_scalar(over[:, :], pk[:, :], float(CAP), FAR, ALU.is_ge, ALU.mult))
                    dve.tensor_tensor(slot[:, quad // 2, :],
                                      over[:, :], base[:, :], ALU.add)
                    link(dve.tensor_tensor(wk[:, :, :, :], hot[:, :, :, :],
                                           wts[:, :, :].unsqueeze(3).to_broadcast([P, 2, 2, E]), ALU.mult))
                    dve.tensor_tensor(rows[:, (quad + 2) % 4:(quad + 2) % 4 + 2, W_COL:W_COL + E], wk[:, :, 0, :], wk[:, :, 1, :],
                                      ALU.add).then_inc(s_slot, 1)
                    done()
                if c:
                    dve.wait_ge(s_proj, i - 1)
                    ht = h_all[:, bass.ds(i - 2, 1), :].rearrange("p a d -> p (a d)")
                    dve.tensor_tensor(ht, bank[6][:, 0:D], ht, ALU.add).then_inc(s_res, 1)
                    dve.wait_ge(s_ones, 1)
                    dve.wait_ge(s_res, i - 1)
                    dve.bn_stats(st2[:, :], ht).then_inc(s_st2, 1)
                    dve.wait_ge(s_ones, 1)
                    dve.wait_ge(s_st2, i - 1)
                    dve.bn_aggr(mv2[:, :], st2[:, :]).then_inc(s_mv2, 1)
                    dve.wait_ge(s_mv2, i - 1)
                    if i0 >= 3:
                        dve.wait_ge(s_rstd2, i - 2)
                    dve.tensor_scalar(ve2[:, :], mv2[:, 1:2], LN_EPS, None, ALU.add).then_inc(s_var2, 1)
                    done()
                if i0 < 3:
                    statistics(2 + i0)

            pipeline(dve, iteration)

            def scale(e, e0, par):
                dve.wait_ge(s_zs[par], 8 * (e - par) + 16)
                if e0 >= 1:
                    dve.wait_ge(s_zt, 2 * e)
                dve.tensor_copy(tok[:, bass.ds(e, 1), :], zs[:, par:par + 1, :, ID_COL]).then_inc(s_tok, 1)
                rms = zs[:, par, :, RMS_COL:RMS_COL + 1]
                dve.tensor_tensor(zn0[:, :, :], zs[:, par, :, 0:D0], rms.to_broadcast([CR, CC, D0]),
                                  ALU.mult).then_inc(s_zn, 1)
                dve.tensor_tensor(zn1[:, :, :, :], zs[:, par, :, D0:D].unsqueeze(2).to_broadcast([CR, CC, 2, D1]),
                                  rms.unsqueeze(3).to_broadcast([CR, CC, 2, D1]), ALU.mult).then_inc(s_zn, 1)

            def split_rest(par, e, n):
                dve.wait_ge(s_wh, 2 * e + (n + 1))
                if n == 0:
                    dve.tensor_tensor(wal[:, par, :], rawa_sb[:, :], wah[:, par, :].bitcast(F32), ALU.subtract).then_inc(s_wl, 1)
                else:
                    dve.tensor_tensor(wbl[:, par, :], rawb_sb[0:D1, :], wbh[0:D1, par, :].bitcast(F32),
                                      ALU.subtract).then_inc(s_wl, 1)

            def z_rest(e, par):
                dve.wait_ge(s_zh, 2 * e + 1)
                dve.scalar_tensor_tensor(z0l[:, par, :], bank[4][:, 0:CAP], nw0_sb[:, bass.ds(e, 1)],
                                         z0h[:, par, :].bitcast(F32), ALU.mult, ALU.subtract).then_inc(s_z, 1)
                dve.wait_ge(s_zh, 2 * e + 2)
                low = z1[D1:P, par, :]
                dve.scalar_tensor_tensor(low, bank[5][D1:P, 0:CAP], nw1_sb[D1:P, bass.ds(e, 1)],
                                         low.bitcast(F32), ALU.mult, ALU.subtract).then_inc(s_z, 1)

            def expert(e, e0, par, more):
                for m in range(MH):
                    dve.wait_ge(s_silu, MH * e + m + 1)
                    if e0 >= 1 and m == 0:
                        dve.wait_ge(s_down, 2 * e)
                    dve.tensor_tensor(hT[:, m, :], sg[:, m % 2, :], bank[2 * (m % 2) + 1][:, 0:CAP],
                                      ALU.mult).then_inc(s_hT, 1)
                    if more and m == 1:
                        scale(e + 1, e0 + 1, 1 - par)
                    if more and 1 <= m <= 2:
                        split_rest(1 - par, e + 1, m - 1)
                if more:
                    z_rest(e + 1, 1 - par)
                for r in range(2):
                    dve.wait_ge(s_down, 2 * e + r + 1)
                    if e0 >= 1 and r == 0:
                        dve.wait_ge(s_yw, CC * e)
                    dve.tensor_tensor(yx[:, 2 * r:2 * r + 2, :],
                                      bank[6 + r][0:CR, 0:2 * D].rearrange("p (a d) -> p a d", a=2),
                                      zs[:, par, 2 * r:2 * r + 2, 0:D], ALU.add).then_inc(s_yx, 1)

            for n in range(2):
                split_rest(0, 0, n)
            scale(0, 0, 0)
            z_rest(0, 0)
            expert(0, 0, 0, True)
            expert(1, 1, 1, True)
            with dve.Fori(1, E // 2 - 1) as pair:
                expert(pair * 2, 2, 0, True)
                expert(pair * 2 + 1, 3, 1, True)
            expert(E - 2, E - 2, 0, True)
            expert(E - 1, E - 1, 1, False)

        @block.gpsimd
        def _(pool):
            pool.memset(h_all[32:64, :, :], 0.0).then_inc(s_gaps, 1)
            pool.memset(h_all[96:P, :, :], 0.0).then_inc(s_gaps, 1)
            pool.wait_ge(s_gaps, 2)
            pool.memset(zero_sb[:, :, :], 0.0).then_inc(s_zeroed, 1)

            def rstd(g):
                pool.wait_ge(s_stat, g + 1)
                lo, hi = STAT_TILES[g]
                pool.tensor_tensor(rstd1[:, lo:hi], ve1[:, lo:hi], small_sb[:, POW0:POW0 + hi - lo],
                                   ALU.pow).then_inc(s_rstd1, 1)

            pool.wait_ge(s_small, 16)
            for g in range(2):
                rstd(g)
            pool.wait_ge(s_zeroed, 1)
            pool.tensor_copy(zero_sb[:, :, ID_COL], small_sb[:, SPARE0:SPARE0 + SPP]).then_inc(s_zero, 1)
            pool.wait_ge(s_zero, 1)
            pool.wait_ge(s_fused_in, 32)
            pool.dma_start(slots.rearrange("(p r) c -> p r c", p=P), zero_sb[:, :, :]).then_inc(s_disp, 16)
            def iteration(i, half, i0, quad, a, b, c, d, m, r1, r2):
                par = quad % 2
                if a:
                    pool.wait_ge(s_rope, i + 1)
                    if i0 >= 1:
                        pool.wait_ge(s_qkt, 2 * i)
                    if i0 == PEEL:
                        pool.wait_ge(s_hots, half - 2)
                        pool.wait_ge(s_rowx, i - 5)
                    for r in (1, 0):
                        pool.tensor_tensor(qk[:, r, :, 0:HD],
                                           rc[:, r * D:(r + 1) * D].rearrange("p (h d) -> p h d", d=HD),
                                           rs[:, r * D:(r + 1) * D].rearrange("p (h d) -> p h d", d=HD),
                                           ALU.add).then_inc(s_qk, 1)
                if i0 < 3:
                    rstd(2 + i0)
                if d:
                    q = 1 - par
                    pool.wait_ge(s_ssq, i - 2)
                    pool.tensor_tensor(ms[:, q:q + 1], ssq[:, q:q + 1], small_sb[:, EPS0:EPS0 + 1],
                                       ALU.add).then_inc(s_ms, 1)
                    pool.wait_ge(s_ms, i - 2)
                    if i0 >= 6:
                        pool.wait_ge(s_disp, 32 * (i - 6) + 16)
                        pool.wait_ge(s_ms, i - 2)
                    r = (quad + 1) % 4
                    pool.tensor_copy(rows[:, r, ID_COL:ID_COL + 1], small_sb[:, bass.ds(i + (IDS0 - 3), 1)])
                    pool.tensor_tensor(rows[:, r, RMS_COL:RMS_COL + 1], ms[:, q:q + 1],
                                       small_sb[:, POW0:POW0 + 1], ALU.pow).then_inc(s_rms, 1)
                if c:
                    pool.wait_ge(s_var2, i - 1)
                    if i0 >= 3:
                        pool.wait_ge(s_x2, i - 2)
                    pool.tensor_tensor(rstd2[:, :], ve2[:, :], small_sb[:, POW0:POW0 + 1],
                                       ALU.pow).then_inc(s_rstd2, 1)
                if i0 == PEEL:
                    pool.wait_ge(s_disp, 16)
                for t, q in ([(i - 6, par)] if i0 >= 6 else []) + ([(i - 5, 1)] if i0 == NT + 4 else []):
                    pool.wait_ge(s_ones, 1)
                    pool.wait_ge(s_slot, half - 2)
                    pool.wait_ge(s_rms, t + 1)
                    pool.wait_ge(s_rowx, t + 1)
                    for k in range(2):
                        pool.indirect_dma_start(
                            out=slots, out_offset=bass.IndirectOffsetOnAxis(
                                ap=slot[:, quad // 2, 2 * q + k:2 * q + k + 1], axis=0),
                            in_=rows[:, (quad + 2 + (q - par)) % 4, :], in_offset=None,
                            bounds_check=E * CAP - 1, oob_is_err=False).then_inc(s_disp, 16)

            pipeline(pool, iteration)

            pool.wait_ge(s_h_out, 80)
            for e in range(E):
                pool.wait_ge(s_tok, e + 1)
                if e >= 1:
                    pool.wait_ge(s_add, 64 * e)
                for c in range(CC):
                    pool.wait_ge(s_yw, CC * e + c + 1)
                    pool.indirect_dma_start(
                        out=out, out_offset=bass.IndirectOffsetOnAxis(ap=tok[:, e, c:c + 1], axis=0),
                        in_=yw[:, c, :], in_offset=None,
                        bounds_check=N + CAP - 1, oob_is_err=True, compute_op=ALU.add).then_inc(s_add, 16)
            pool.wait_ge(s_add, 64 * E)


_INS = ["patches", "txt", "posb", "tokb", "tokw", "wqkv", "wo", "gate", "w13", "w2", "normw",
        "rope", "mask", "small", "order", "ident"]


def kernel(x, txt, L0_tok_W, L0_tok_b, L0_tok_pos_emb, L0_attn_Wq, L0_attn_bq, L0_attn_Wk, L0_attn_bk,
           L0_attn_Wv, L0_attn_bv, L0_attn_Wo, L0_attn_bo, L0_ffn_gate_w, L0_ffn_w13, L0_ffn_w2,
           L0_ffn_norm_w):
    import concourse.bacc as bacc
    from concourse.bass_utils import run_bass_kernel_spmd

    g = IMG // PATCH
    a = {k: np.asarray(v) for k, v in locals().copy().items() if isinstance(v, np.ndarray) or hasattr(v, "dtype")}
    flat = a["x"].reshape(B, g, PATCH, g, PATCH, CH).transpose(2, 4, 5, 0, 1, 3).reshape(PK, P, B * NPATCH)
    arrays = {
        "patches": flat.transpose(1, 0, 2),
        "txt": a["txt"],
        "posb": np.tile(a["L0_tok_pos_emb"], (P // NPATCH, 1)),
        "tokb": np.tile(a["L0_tok_b"][None, :], (P, 1)),
        "tokw": a["L0_tok_W"].reshape(PK, P, D).transpose(1, 0, 2),
        "wqkv": np.concatenate([
            np.concatenate([a["L0_attn_Wq"], a["L0_attn_Wk"], a["L0_attn_Wv"]], axis=1),
            np.concatenate([a["L0_attn_bq"], a["L0_attn_bk"], a["L0_attn_bv"]])[None, :]], axis=0),
        "wo": np.concatenate([a["L0_attn_Wo"], a["L0_attn_bo"][None, :]], axis=0),
        "gate": a["L0_ffn_gate_w"].T,
        "w13": a["L0_ffn_w13"].transpose(0, 2, 1).reshape(E * D, 2 * H),
        "w2": a["L0_ffn_w2"].transpose(0, 2, 1).reshape(E * H, D),
        "normw": a["L0_ffn_norm_w"].T,
        **shape_constants(),
    }
    nc = bacc.Bacc("TRN2", target_bir_lowering=False, num_devices=1)
    feeds, args = {}, []
    for name in _INS:
        arr = np.ascontiguousarray(arrays[name])
        feeds[f"in_{name}"] = arr
        args.append(nc.dram_tensor(f"in_{name}", arr.shape, mybir.dt.from_np(arr.dtype), kind="ExternalInput").ap())
    args.append(nc.dram_tensor("out_rows", (N + CAP, D), F32, kind="ExternalOutput").ap())
    build(nc, *args)
    got = run_bass_kernel_spmd(nc, [feeds], core_ids=[0]).results[0]["out_rows"]
    return got[:N].reshape(B, S, D)
```
